# Optimizing a Trainium2 kernel written in Bass

```python
import numpy as np
import jax
import jax.numpy as jnp

def _softmax(x, axis=-1):
    return jax.nn.softmax(x, axis=axis)

def _gelu(x):
    return jax.nn.gelu(x, approximate=True)

def _silu(x):
    return jax.nn.silu(x)

def _sigmoid(x):
    return jax.nn.sigmoid(x)

def _layernorm(x, axis=-1, eps=1e-05):
    m = jnp.mean(x, axis=axis, keepdims=True)
    v = jnp.var(x, axis=axis, keepdims=True)
    return (x - m) / jnp.sqrt(v + eps)

def _scatter_add(tgt, idx, src, axis=0):
    return tgt.at[idx].add(src)

def _segment_sum(src, seg, n):
    return jax.ops.segment_sum(src, seg, n)
kernel_name = 'mk_prb_d1_jaxref_r4_e6328b'

def setup_inputs(seed: int=0):
    np.random.seed(seed)
    _w = jnp.asarray

    def _L0_attn_setup():
        import jax, jax.numpy as jnp
        import numpy as np
        D_CONV = 4
        DT_RANK = 64
        D_STATE = 16

        def _selective_scan(u, delta, A, Bm, Cm, D):
            b, l, d = u.shape
            n = A.shape[1]
            deltaA = jnp.exp(jnp.einsum('bld,dn->bldn', delta, A))
            dBu = delta[..., None] * Bm[:, :, None, :] * u[..., None]

            def step(state, inp):
                dA_t, dBu_t, C_t = inp
                state = dA_t * state + dBu_t
                y_t = jnp.einsum('bdn,bn->bd', state, C_t)
                return (state, y_t)
            init = jnp.zeros((b, d, n), u.dtype)
            xs = (jnp.swapaxes(deltaA, 0, 1), jnp.swapaxes(dBu, 0, 1), jnp.swapaxes(Cm, 0, 1))
            _, ys = jax.lax.scan(step, init, xs)
            y = jnp.swapaxes(ys, 0, 1)
            return y + u * D
        key = jax.random.key(seed)
        ks = jax.random.split(key, 10)
        d_model, d_in, L, B = (256, 512, 256, 2)
        s = 0.02
        x = jax.random.normal(ks[0], (B, L, d_model), jnp.float32)
        W_in = jax.random.normal(ks[1], (d_model, 2 * d_in), jnp.float32) * s
        conv_w = jax.random.normal(ks[2], (D_CONV, 1, d_in), jnp.float32) * s
        conv_b = jax.random.normal(ks[3], (d_in,), jnp.float32) * s
        W_x = jax.random.normal(ks[4], (d_in, DT_RANK + 2 * D_STATE), jnp.float32) * s
        W_dt = jax.random.normal(ks[5], (DT_RANK, d_in), jnp.float32) * s
        b_dt = jax.random.normal(ks[6], (d_in,), jnp.float32) * s
        A_log = jnp.log(jnp.tile(jnp.arange(1, D_STATE + 1, dtype=jnp.float32), (d_in, 1)))
        D = jnp.ones((d_in,), jnp.float32)
        W_out = jax.random.normal(ks[7], (d_in, d_model), jnp.float32) * s
        return {'x': x, 'W_in': W_in, 'conv_w': conv_w, 'conv_b': conv_b, 'W_x': W_x, 'W_dt': W_dt, 'b_dt': b_dt, 'A_log': A_log, 'D': D, 'W_out': W_out}
    _L0_attn_in = _L0_attn_setup()

    def _L0_ffn_setup():
        import jax, jax.numpy as jnp
        import numpy as np
        S, B, D = (256, 2, 256)
        E, TOPK = (15, 3)
        F = 256
        FS = 512

        def _uinit(k, shape, out_dim):
            std = out_dim ** (-0.5)
            return jax.random.uniform(k, shape, jnp.float32, -std, std)
        key = jax.random.key(seed)
        ks = jax.random.split(key, 10)
        return {'x': jax.random.normal(ks[0], (S, B, D), jnp.float32), 'gate_w': jax.random.normal(ks[1], (E, D), jnp.float32) * D ** (-0.5), 'fc1_w': _uinit(ks[2], (E, 2 * F, D), 2 * F), 'fc1_b': _uinit(ks[3], (E, 2 * F), 2 * F), 'geglu_mult': jnp.ones((E, F), jnp.float32), 'fc2_w': _uinit(ks[4], (E, D, F), D), 'fc2_b': _uinit(ks[5], (E, D), D), 's_fc1_w': _uinit(ks[6], (2 * FS, D), 2 * FS), 's_fc1_b': _uinit(ks[7], (2 * FS,), 2 * FS), 's_geglu_mult': jnp.ones((FS,), jnp.float32), 's_fc2_w': _uinit(ks[8], (D, FS), D), 's_fc2_b': _uinit(ks[9], (D,), D)}
    _L0_ffn_in = _L0_ffn_setup()
    _d = {'L0_attn_x': _L0_attn_in['x'], 'L0_attn_W_in': _L0_attn_in['W_in'], 'L0_attn_conv_w': _L0_attn_in['conv_w'], 'L0_attn_conv_b': _L0_attn_in['conv_b'], 'L0_attn_W_x': _L0_attn_in['W_x'], 'L0_attn_W_dt': _L0_attn_in['W_dt'], 'L0_attn_b_dt': _L0_attn_in['b_dt'], 'L0_attn_A_log': _L0_attn_in['A_log'], 'L0_attn_D': _L0_attn_in['D'], 'L0_attn_W_out': _L0_attn_in['W_out'], 'L0_ffn_gate_w': _L0_ffn_in['gate_w'], 'L0_ffn_fc1_w': _L0_ffn_in['fc1_w'], 'L0_ffn_fc1_b': _L0_ffn_in['fc1_b'], 'L0_ffn_geglu_mult': _L0_ffn_in['geglu_mult'], 'L0_ffn_fc2_w': _L0_ffn_in['fc2_w'], 'L0_ffn_fc2_b': _L0_ffn_in['fc2_b'], 'L0_ffn_s_fc1_w': _L0_ffn_in['s_fc1_w'], 'L0_ffn_s_fc1_b': _L0_ffn_in['s_fc1_b'], 'L0_ffn_s_geglu_mult': _L0_ffn_in['s_geglu_mult'], 'L0_ffn_s_fc2_w': _L0_ffn_in['s_fc2_w'], 'L0_ffn_s_fc2_b': _L0_ffn_in['s_fc2_b']}
    _x0 = _d['L0_attn_x']
    _d['L0_attn_x'] = jax.random.normal(jax.random.fold_in(jax.random.key(seed), 1), (2, 2048, 256), dtype=_x0.dtype)
    del _x0
    return _d

def reference(L0_attn_x, L0_attn_W_in, L0_attn_conv_w, L0_attn_conv_b, L0_attn_W_x, L0_attn_W_dt, L0_attn_b_dt, L0_attn_A_log, L0_attn_D, L0_attn_W_out, L0_ffn_gate_w, L0_ffn_fc1_w, L0_ffn_fc1_b, L0_ffn_geglu_mult, L0_ffn_fc2_w, L0_ffn_fc2_b, L0_ffn_s_fc1_w, L0_ffn_s_fc1_b, L0_ffn_s_geglu_mult, L0_ffn_s_fc2_w, L0_ffn_s_fc2_b):

    def _L0_attn_ref(x, W_in, conv_w, conv_b, W_x, W_dt, b_dt, A_log, D, W_out):
        import jax, jax.numpy as jnp
        import numpy as np
        D_CONV = 4
        DT_RANK = 64
        D_STATE = 16

        def _selective_scan(u, delta, A, Bm, Cm, D):
            b, l, d = u.shape
            n = A.shape[1]
            deltaA = jnp.exp(jnp.einsum('bld,dn->bldn', delta, A))
            dBu = delta[..., None] * Bm[:, :, None, :] * u[..., None]

            def step(state, inp):
                dA_t, dBu_t, C_t = inp
                state = dA_t * state + dBu_t
                y_t = jnp.einsum('bdn,bn->bd', state, C_t)
                return (state, y_t)
            init = jnp.zeros((b, d, n), u.dtype)
            xs = (jnp.swapaxes(deltaA, 0, 1), jnp.swapaxes(dBu, 0, 1), jnp.swapaxes(Cm, 0, 1))
            _, ys = jax.lax.scan(step, init, xs)
            y = jnp.swapaxes(ys, 0, 1)
            return y + u * D
        B, L, _ = x.shape
        d_in = W_in.shape[1] // 2
        x_and_res = x @ W_in
        x_, res = jnp.split(x_and_res, [d_in], axis=-1)
        x_pad = jnp.pad(x_, ((0, 0), (D_CONV - 1, 0), (0, 0)))
        x_conv = jax.lax.conv_general_dilated(x_pad, conv_w, window_strides=(1,), padding='VALID', dimension_numbers=('NWC', 'WIO', 'NWC'), feature_group_count=d_in)
        x_conv = x_conv[:, :L, :] + conv_b
        x_conv = jax.nn.silu(x_conv)
        A = -jnp.exp(A_log)
        x_dbl = x_conv @ W_x
        delta, Bm, Cm = jnp.split(x_dbl, [DT_RANK, DT_RANK + D_STATE], axis=-1)
        delta = jax.nn.softplus(delta @ W_dt + b_dt)
        y = _selective_scan(x_conv, delta, A, Bm, Cm, D)
        y = y * jax.nn.silu(res)
        return y @ W_out

    def _L0_ffn_ref(x, gate_w, fc1_w, fc1_b, geglu_mult, fc2_w, fc2_b, s_fc1_w, s_fc1_b, s_geglu_mult, s_fc2_w, s_fc2_b):
        import jax, jax.numpy as jnp
        import numpy as np
        S, B, D = (256, 2, 256)
        E, TOPK = (15, 3)
        F = 256
        FS = 512

        def _uinit(k, shape, out_dim):
            std = out_dim ** (-0.5)
            return jax.random.uniform(k, shape, jnp.float32, -std, std)
        s, b, d = x.shape
        xt = x.reshape(-1, d)
        T = xt.shape[0]
        logits = xt @ gate_w.T
        scores = jax.nn.softmax(logits, axis=-1)
        topk_w, topk_idx = jax.lax.top_k(scores, TOPK)
        topk_w = topk_w / (jnp.sum(topk_w, axis=-1, keepdims=True) + 1e-20)
        comb = jnp.zeros((T, E), xt.dtype).at[jnp.arange(T)[:, None], topk_idx].add(topk_w)
        h = jnp.einsum('td,efd->etf', xt, fc1_w) + fc1_b[:, None, :]
        xh, g = (h[..., :F], h[..., F:])
        a = jax.nn.gelu(g, approximate=False) * xh * geglu_mult[:, None, :]
        yexp = jnp.einsum('etf,edf->etd', a, fc2_w) + fc2_b[:, None, :]
        y = jnp.einsum('etd,te->td', yexp, comb)
        hs = xt @ s_fc1_w.T + s_fc1_b
        xs, gs = (hs[..., :FS], hs[..., FS:])
        as_ = jax.nn.gelu(gs, approximate=False) * xs * s_geglu_mult
        ys = as_ @ s_fc2_w.T + s_fc2_b
        return (y + ys).reshape(s, b, d)
    x = L0_attn_x
    xn = _layernorm(x, axis=-1)
    x = x + _L0_attn_ref(xn, L0_attn_W_in, L0_attn_conv_w, L0_attn_conv_b, L0_attn_W_x, L0_attn_W_dt, L0_attn_b_dt, L0_attn_A_log, L0_attn_D, L0_attn_W_out) + _L0_ffn_ref(xn, L0_ffn_gate_w, L0_ffn_fc1_w, L0_ffn_fc1_b, L0_ffn_geglu_mult, L0_ffn_fc2_w, L0_ffn_fc2_b, L0_ffn_s_fc1_w, L0_ffn_s_fc1_b, L0_ffn_s_geglu_mult, L0_ffn_s_fc2_w, L0_ffn_s_fc2_b)
    return x

_drawn_inputs = setup_inputs


def setup_inputs(seed=0):
    import zlib

    import numpy as np

    out = dict(_drawn_inputs(seed))
    spreads = {'L0_attn_D': (1.0, 0.6),
     'L0_ffn_geglu_mult': (1.0, 0.6),
     'L0_ffn_s_geglu_mult': (1.0, 0.6)}
    factors = {'L0_attn_W_in': 8.0,
     'L0_attn_conv_w': 8.0,
     'L0_attn_conv_b': 8.0,
     'L0_attn_W_x': 8.0,
     'L0_attn_W_dt': 8.0,
     'L0_attn_b_dt': 8.0,
     'L0_attn_A_log': 8.0,
     'L0_attn_W_out': 8.0,
     'L0_ffn_fc1_b': 64.0,
     'L0_ffn_s_fc1_b': 64.0,
     'L0_ffn_gate_w': 8.0,
     'L0_ffn_fc1_w': 8.0,
     'L0_ffn_fc2_w': 8.0,
     'L0_ffn_fc2_b': 64.0,
     'L0_ffn_s_fc1_w': 8.0,
     'L0_ffn_s_fc2_w': 8.0,
     'L0_ffn_s_fc2_b': 64.0}
    for name, (base, spread) in spreads.items():
        noise = np.random.default_rng([zlib.crc32(name.encode()), seed]).standard_normal(out[name].shape)
        drawn = base * np.exp(spread * noise) if base else spread * noise
        out[name] = jnp.asarray(drawn.astype(out[name].dtype))
    for name, factor in factors.items():
        out[name] = (out[name] * factor).astype(out[name].dtype)
    return out
```

```python
import concourse.bass as bass
from concourse import mybir
from contextlib import ExitStack


def mamba_moe_block(nc, x, w_in, conv_w, conv_b, w_x, w_dt, b_dt, a_log, d_skip, w_out, gate_w,
                    fc1, fc1_b, mult, fc2, fc2_b, ident_in, prio_in, out):
    fp32 = mybir.dt.float32
    u32 = mybir.dt.uint32
    ALU = mybir.AluOpType
    ACT = mybir.ActivationFunctionType
    AX = mybir.AxisListType

    P = 128
    B, L, DM = x.shape
    KM = DM // P
    DIN = w_out.shape[1] * P
    ND = DIN // P
    R = w_dt.shape[0]
    N = a_log.shape[1] // ND
    XD = w_x.shape[2]
    TAPS = conv_w.shape[2]
    HALO = TAPS - 1
    TC = 512
    NT = TC // P
    CPB = L // TC
    E = gate_w.shape[2]
    TOPK = 3
    UNITS = fc1.shape[0]
    NF = fc2.shape[2]
    F = NF * P
    NS = 2
    NG = N // NS
    assert UNITS == 2 * NG + 1 == E + 2 and B * L % TC == 0 and NG % 2 == 0

    xs = x.rearrange("b (c t p) d -> b c p t d", p=P, t=NT)
    outs = out.rearrange("b (c t p) d -> b c p t d", p=P, t=NT)
    bc_dram = nc.dram_tensor("bc_rows", [2, 2, N, TC], fp32, kind="Internal").ap()

    ctx = ExitStack()
    with ctx:
        def sb(name, shape, dt=fp32):
            return ctx.enter_context(nc.sbuf_tensor(name, shape, dt))

        def pb(name):
            return ctx.enter_context(nc.psum_tensor(name, [P, 512], fp32))

        def sem(name):
            return ctx.enter_context(nc.semaphore(name))

        ident = sb("ident", [P, P])
        prio = sb("prio", [P, NT, E])
        win = sb("win", [P, KM, 2 * DIN])
        wx = sb("wx", [P, ND, XD])
        wdt = sb("wdt", [R, DIN])
        wout = sb("wout", [P, ND, DM])
        gw = sb("gw", [P, KM, E])
        cw = sb("cw", [P, ND, TAPS])
        cb = sb("cb", [P, ND])
        bdt = sb("bdt", [P, ND])
        al = sb("al", [P, ND * N])
        am = sb("am", [P, ND * N])
        dsk = sb("dsk", [P, ND])
        dskip = sb("dskip", [P, ND, P])
        b1 = sb("b1", [P, UNITS * 2 * NF])
        mu = sb("mu", [P, UNITS * NF])
        b2 = sb("b2", [E + 1, DM])
        xa = sb("xa", [P, 2, NT, DM])
        xn = sb("xn", [P, NT, DM])
        st = sb("st", [P, NT, 6])
        mv = sb("mv", [P, NT, 2])
        var = sb("var", [P, NT])
        dev = sb("dev", [P, NT])
        rstd = sb("rstd", [P, NT])
        xnT = sb("xnT", [P, KM, TC])
        xr = sb("xr", [P, ND, HALO + TC])
        sres = sb("sres", [P, ND, TC])
        cv = sb("cv", [P, ND, TC])
        u = sb("u", [P, ND, TC])
        delta = sb("delta", [P, ND, TC])
        du = sb("du", [P, ND, TC])
        xdb = sb("xdb", [XD, TC])
        spx = sb("spx", [P, 2, TC])
        spe = sb("spe", [P, 2, TC])
        spl = sb("spl", [P, 2, TC])
        spq = sb("spq", [P, TC])
        spm = sb("spm", [P, TC], u32)
        lg = sb("lg", [P, NT, E])
        sc = sb("sc", [P, NT, E])
        sm = sb("sm", [P, NT, E])
        eq = sb("eq", [P, NT, E])
        r4 = sb("r4", [P, NT])
        r5 = sb("r5", [P, NT])
        comb = sb("comb", [P, NT * (E + 1)])
        combT = sb("combT", [E + 1, TC])
        Bb = [sb(f"Bb{i}", [P, NS, TC]) for i in range(2)]
        Cb = [sb(f"Cb{i}", [P, NS, TC]) for i in range(2)]
        dA = [sb(f"dA{i}", [P, NS, TC]) for i in range(2)]
        dBu = sb("dBu", [P, NS, TC])
        h = [sb(f"h{i}", [P, NS, TC]) for i in range(2)]
        hC = [sb(f"hC{i}", [P, NS, TC]) for i in range(2)]
        state = sb("state", [P, ND * N])
        w1 = [sb(f"w1_{s}", [P, KM, 2 * F]) for s in "ABS"]
        w2 = [sb(f"w2_{s}", [P, NF, DM]) for s in "ABS"]
        act = [sb(f"act_{s}", [P, NF, TC]) for s in "ABS"]

        y = [pb(f"y{i}") for i in range(4)]
        fh = [pb(f"fh{i}") for i in range(3)]
        po = pb("po")

        s_const = sem("constants_loaded")
        s_am = sem("decay_exponentiated")
        s_init = sem("constants_made")
        s_x = sem("x_loaded")
        s_bcd = sem("bc_rows_stored")
        s_bcl = [sem(f"bc_spread_{i}") for i in range(2)]
        s_w = [sem(f"unit_weights_{s}") for s in "ABS"]
        s_out = sem("out_stored")
        s_v = sem("vector_front_steps")
        s_mark = sem("waits_taken")
        s_zero = sem("batch_zeroed")
        s_var = sem("variance_ready")
        s_sd = sem("deviation_ready")
        s_xn = sem("xn_ready")
        s_T = sem("xn_transposed")
        s_xnT = sem("xnT_copied")
        s_lg = sem("logits_ready")
        s_lsub = sem("logits_shifted")
        s_lexp = sem("logits_exponentiated")
        s_comb = sem("weights_ready")
        s_ct = sem("weights_transposed")
        s_ctc = sem("weightsT_copied")
        s_ip = sem("inproj_ready")
        s_ipc = sem("inproj_copied")
        s_cv = sem("conv_ready")
        s_halo = sem("halo_kept")
        s_u = sem("u_ready")
        s_xd = sem("xdbl_ready")
        s_xdc = sem("xdbl_copied")
        s_dt = sem("dt_ready")
        s_spab = sem("softplus_abs")
        s_spe = sem("softplus_exp")
        s_spl = sem("softplus_log")
        s_dl = sem("delta_ready")
        s_du = sem("du_ready")
        s_dA = sem("dA_ready")
        s_dBu = sem("dBu_ready")
        s_h = sem("h_ready")
        s_st = sem("state_kept")
        s_hC = sem("hC_ready")
        s_ns = sem("y_accumulated")
        s_yg = sem("y_gated")
        s_f1 = sem("fc1_tile_ready")
        s_g = sem("gelu_ready")
        s_a = sem("product_ready")
        s_w2 = sem("fc2_scaled")
        s_o = sem("out_psum_ready")
        s_oc = sem("out_psum_added")

        OUSE = 2 + 2 * UNITS + 2
        G = ND * NG
        NCONST = 15 * 16
        CR = 2 * ND

        HS = 1
        INIT = 2 + ND
        VSTEPS = 72

        def ybank(j):
            return y[(3, 0, 1)[j % 3]]

        def spread(r):
            return r[:, :].unsqueeze(2).to_broadcast([P, NT, E])

        block = ctx.enter_context(nc.Block())

        def plain(eng):
            eng.sem_inc(s_mark, 1)

        def chunks(eng):
            with eng.Fori(0, B) as b:
                for cc in range(CPB):
                    yield b * CPB + cc, b, cc

        def groups(eng):
            plain(eng)
            with eng.Fori(0, NG // 2) as i:
                for q in range(2):
                    yield i * 2 + q, q

        @block.sync
        def _(sp):
            for t, src in ((ident, ident_in), (prio, prio_in), (win, w_in), (wx, w_x), (wdt, w_dt),
                           (wout, w_out), (gw, gate_w), (cw, conv_w), (cb, conv_b), (bdt, b_dt),
                           (al, a_log), (dsk, d_skip), (b1, fc1_b), (mu, mult), (b2, fc2_b)):
                dims = (slice(None),) * len(t.shape)
                sp.dma_start(t[dims], src[dims]).then_inc(s_const, 16)

            def unit(slot, index, added):
                sp.wait_ge(s_oc, added + HS)
                sp.dma_start(w1[slot][:, :, :], fc1[bass.ds(index, 1)].rearrange("a p k f -> p (a k) f"))\
                    .then_inc(s_w[slot], 16)
                sp.dma_start(w2[slot][:, :, :], fc2[bass.ds(index, 1)].rearrange("a p k f -> p (a k) f"))\
                    .then_inc(s_w[slot], 16)

            def store(c, b, cc):
                sp.wait_ge(s_oc, (c + 1) * OUSE + HS)
                sp.dma_start(outs[bass.ds(b, 1), cc].rearrange("a p t d -> (a p) t d"), xa[:, cc % 2, :, :])\
                    .then_inc(s_out, 16)
                sp.wait_ge(s_out, (c + 1) * 16)
                plain(sp)

            for c, b, cc in chunks(sp):
                sp.dma_start(xa[:, cc % 2, :, :], xs[bass.ds(b, 1), cc].rearrange("a p t d -> (a p) t d"))\
                    .then_inc(s_x, 16)
                if cc > 0:
                    store(c - 1, b, cc - 1)
                unit(2, UNITS - 1, c * OUSE)
                sp.wait_ge(s_xdc, c + 1)
                sp.dma_start(bc_dram[cc % 2].rearrange("s n t -> (s n) t"), xdb[R:XD, :]).then_inc(s_bcd, 16)
                sp.wait_ge(s_bcd, (c + 1) * 16 + HS)
                for n, q in groups(sp):
                    g = c * NG + n
                    sp.wait_ge(s_h, (g - 1) * ND + CR)
                    sp.wait_ge(s_hC, (g - 1) * ND + CR)
                    for k, t in enumerate((Bb, Cb)):
                        sp.dma_start(t[q][:, :, :], bc_dram[cc % 2, k, bass.ds(n * NS, NS), :]
                                     .partition_broadcast(P)).then_inc(s_bcl[q], 16)
                    unit(0, n * 2, c * OUSE + n * 4)
                    unit(1, n * 2 + 1, c * OUSE + n * 4 + 2)
                if cc == CPB - 1:
                    store(c, b, cc)

        @block.tensor
        def _(pe):
            pe.wait_ge(s_const, NCONST)
            pe.wait_ge(s_init, INIT)

            def fc1_unit(slot, w, use):
                pe.wait_ge(s_w[slot], (use + 1) * 32)
                pe.wait_ge(s_g, w * NF + HS)
                pe.wait_ge(s_a, w * NF + HS)
                for k, ft in enumerate((NF, NF + 1, 0, 1)):
                    if k == 3:
                        pe.wait_ge(s_g, w * NF + 1 + HS)
                    for m in range(KM):
                        mm = pe.matmul(fh[k % 3][:, :], w1[slot][:, m, ft * P:(ft + 1) * P], xnT[:, m, :],
                                       start=(m == 0), stop=(m == KM - 1))
                    mm.then_inc(s_f1, 1)

            def fc2_half(slot, w, o, half):
                if half == 0:
                    pe.wait_ge(s_a, (w + 1) * NF + HS)
                    pe.wait_ge(s_w2, w + 1)
                pe.wait_ge(s_oc, o + HS)
                for t in range(2):
                    tok = (half * 2 + t) * P
                    for f in range(NF):
                        mm = pe.matmul(po[:, t * DM:(t + 1) * DM], act[slot][:, f, tok:tok + P], w2[slot][:, f, :],
                                       start=(f == 0), stop=(f == NF - 1))
                mm.then_inc(s_o, 1)

            def state_sum(d, k):
                pe.wait_ge(s_hC, k + 1 + CR)
                for i in range(NS):
                    mm = pe.matmul(y[d][:, :], ident[:, :], hC[d % 2][:, i, :], start=False, stop=False,
                                   skip_group_check=True)
                mm.then_inc(s_ns, 1)

            for c, b, cc in chunks(pe):
                pe.wait_ge(s_yg, c * ND + HS)
                for t in range(NT):
                    pe.wait_ge(s_xn, c * NT + t + 1)
                    for m in range(KM):
                        mm = pe.transpose(y[m][:, t * P:(t + 1) * P], xn[:, t, m * P:(m + 1) * P], ident[:, :])
                mm.then_inc(s_T, 1)
                pe.wait_ge(s_xnT, (c + 1) * KM)
                for t in range(NT):
                    for m in range(KM):
                        mm = pe.matmul(y[2][:, t * E:(t + 1) * E], xnT[:, m, t * P:(t + 1) * P], gw[:, m, :],
                                       start=(m == 0), stop=(m == KM - 1))
                mm.then_inc(s_lg, 1)
                for j in range(2 * ND):
                    if j >= 3:
                        pe.wait_ge(s_ipc, c * 2 * ND + j - 2)
                    for m in range(KM):
                        mm = pe.matmul(ybank(j)[:, :], win[:, m, j * P:(j + 1) * P], xnT[:, m, :],
                                       start=(m == 0), stop=(m == KM - 1))
                    mm.then_inc(s_ip, 1)
                pe.wait_ge(s_ipc, (c + 1) * 2 * ND)
                for d in range(ND):
                    pe.wait_ge(s_u, c * ND + d + 1)
                    mm = pe.matmul(y[1][0:XD, :], wx[:, d, :], u[:, d, :], start=(d == 0), stop=(d == ND - 1))
                mm.then_inc(s_xd, 1)
                pe.wait_ge(s_xdc, c + 1)
                for d in range(ND):
                    if d >= 2:
                        pe.wait_ge(s_spab, c * ND + d - 1)
                    pe.matmul(y[(0, 3)[d % 2]][:, :], wdt[:, d * P:(d + 1) * P], xdb[0:R, :],
                              start=True, stop=True).then_inc(s_dt, 1)
                pe.wait_ge(s_comb, c + 1)
                for t in range(NT):
                    mm = pe.transpose(y[2][0:E + 1, t * P:(t + 1) * P], comb[:, t * (E + 1):(t + 1) * (E + 1)],
                                      ident[:, :])
                mm.then_inc(s_ct, 1)
                pe.wait_ge(s_ctc, c + 1)
                for half in range(2):
                    pe.wait_ge(s_oc, c * OUSE + half + HS)
                    for t in range(2):
                        tok = (half * 2 + t) * P
                        mm = pe.matmul(po[:, t * DM:(t + 1) * DM], combT[:, tok:tok + P], b2[:, :],
                                       start=True, stop=True)
                    mm.then_inc(s_o, 1)
                pe.wait_ge(s_spab, (c + 1) * ND)
                for d in range(ND):
                    pe.matmul(y[d][:, :], dskip[:, d, :], u[:, d, :], start=True, stop=False,
                              skip_group_check=True)
                for n, q in groups(pe):
                    g = c * NG + n
                    w = c * UNITS + n * 2
                    o = c * OUSE + 2 + n * 4
                    fc1_unit(0, w, g)
                    state_sum(0, g * ND)
                    state_sum(1, g * ND + 1)
                    fc1_unit(1, w + 1, g)
                    fc2_half(0, w, o, 0)
                    state_sum(2, g * ND + 2)
                    fc2_half(0, w, o + 1, 1)
                    state_sum(3, g * ND + 3)
                    fc2_half(1, w + 1, o + 2, 0)
                    fc2_half(1, w + 1, o + 3, 1)
                w = (c + 1) * UNITS - 1
                o = (c + 1) * OUSE - 4
                fc1_unit(2, w, c)
                fc2_half(2, w, o, 0)
                fc2_half(2, w, o + 1, 1)
                pe.wait_ge(s_yg, (c + 1) * ND + HS)
                for half in range(2):
                    pe.wait_ge(s_oc, o + 2 + half + HS)
                    for t in range(2):
                        tok = (half * 2 + t) * P
                        for d in range(ND):
                            mm = pe.matmul(po[:, t * DM:(t + 1) * DM], cv[:, d, tok:tok + P], wout[:, d, :],
                                           start=(d == 0), stop=(d == ND - 1))
                    mm.then_inc(s_o, 1)

        @block.scalar
        def _(sa):
            sa.wait_ge(s_const, NCONST)
            sa.activation(am[:, :], al[:, :], ACT.Exp).then_inc(s_am, 1)
            sa.wait_ge(s_init, INIT)

            def gelu(slot, w, unit, added):
                sa.wait_ge(s_oc, added + HS)
                for f in range(NF):
                    sa.wait_ge(s_f1, w * 2 * NF + f + 1)
                    sa.activation(act[slot][:, f, :], fh[f][:, :], ACT.Gelu,
                                  bias=b1[:, bass.ds(unit * 2 * NF + NF + f, 1)]).then_inc(s_g, 1)

            for c, b, cc in chunks(sa):
                sa.wait_ge(s_var, c + 1)
                sa.activation(dev[:, :], var[:, :], ACT.Sqrt).then_inc(s_sd, 1)
                sa.wait_ge(s_T, c + 1)
                for m in range(KM):
                    sa.activation(xnT[:, m, :], y[m][:, :], ACT.Copy).then_inc(s_xnT, 1)
                sa.wait_ge(s_halo, c + HS)
                for j in range(ND):
                    sa.wait_ge(s_ip, c * 2 * ND + j + 1)
                    sa.activation(xr[:, j, HALO:], ybank(j)[:, :], ACT.Copy).then_inc(s_ipc, 1)
                for j in range(ND, 2 * ND):
                    sa.wait_ge(s_ip, c * 2 * ND + j + 1)
                    sa.activation(sres[:, j - ND, :], ybank(j)[:, :], ACT.Silu).then_inc(s_ipc, 1)
                for d in range(ND):
                    sa.wait_ge(s_cv, c * ND + d + 1)
                    sa.activation(u[:, d, :], cv[:, d, :], ACT.Silu).then_inc(s_u, 1)
                sa.wait_ge(s_lsub, c + 1)
                sa.activation(lg[:, :, :], lg[:, :, :], ACT.Exp).then_inc(s_lexp, 1)
                sa.wait_ge(s_xd, c + 1)
                sa.wait_ge(s_bcd, c * 16 + HS)
                sa.activation(xdb[:, :], y[1][0:XD, :], ACT.Copy).then_inc(s_xdc, 1)
                for d in range(ND):
                    k = c * ND + d
                    bank = y[(0, 3)[d % 2]]
                    sa.wait_ge(s_dt, k + 1)
                    if d >= 2:
                        sa.wait_ge(s_dl, k - 1)
                    sa.activation(spx[:, d % 2, :], bank[:, :], ACT.Identity, bias=bdt[:, d:d + 1])
                    sa.activation(spe[:, d % 2, :], bank[:, :], ACT.Abs, bias=bdt[:, d:d + 1]).then_inc(s_spab, 1)
                    sa.wait_ge(s_spab, k + 1)
                    sa.activation(spe[:, d % 2, :], spe[:, d % 2, :], ACT.Exp, scale=-1.0).then_inc(s_spe, 1)
                    sa.wait_ge(s_spe, k + 1)
                    sa.activation(spl[:, d % 2, :], spe[:, d % 2, :], ACT.Ln, bias=1.0).then_inc(s_spl, 1)
                sa.wait_ge(s_ct, c + 1)
                sa.activation(combT[:, :], y[2][0:E + 1, :], ACT.Copy).then_inc(s_ctc, 1)
                sa.wait_ge(s_dl, (c + 1) * ND)
                for n, q in groups(sa):
                    g = c * NG + n
                    w = c * UNITS + n * 2
                    for d in range(ND):
                        sa.wait_ge(s_h, g * ND + d - 1 + CR)
                        for i in range(NS):
                            e = sa.activation(dA[d % 2][:, i, :], delta[:, d, :], ACT.Exp,
                                              scale=am[:, bass.ds(n * NS + (d * N + i), 1)])
                        e.then_inc(s_dA, 1)
                    gelu(0, w, n * 2, c * OUSE + n * 4)
                    gelu(1, w + 1, n * 2 + 1, c * OUSE + n * 4 + 2)
                gelu(2, (c + 1) * UNITS - 1, UNITS - 1, c * OUSE)

        @block.gpsimd
        def _(gp):
            gp.sem_inc(s_h, CR)
            gp.sem_inc(s_hC, CR)
            gp.sem_inc(s_ns, CR)
            for q in (s_g, s_a, s_oc, s_yg, s_halo, s_bcd, s_st):
                gp.sem_inc(q, HS)
            gp.memset(comb[:, :], 1.0).then_inc(s_init, 1)
            for c, b, cc in chunks(gp):
                for n, q in groups(gp):
                    g = c * NG + n
                    gp.wait_ge(s_bcl[q], (g - q) * 16 + 32)
                    for d in range(ND):
                        k = g * ND + d
                        gp.wait_ge(s_h, k + 1 + CR)
                        gp.wait_ge(s_ns, k - 1 + CR)
                        gp.tensor_tensor(hC[d % 2][:, :, :], h[d % 2][:, :, :], Cb[q][:, :, :], ALU.mult)\
                            .then_inc(s_hC, 1)

        @block.vector
        def _(dv):
            dv.wait_ge(s_const, NCONST)
            dv.wait_ge(s_am, 1)
            dv.tensor_scalar(am[:, :], am[:, :], -1.0, None, ALU.mult).then_inc(s_init, 1)
            for d in range(ND):
                dv.tensor_scalar(dskip[:, d, :], ident[:, :], dsk[:, d:d + 1], None, ALU.mult).then_inc(s_init, 1)
            dv.wait_ge(s_init, INIT)

            class Front:
                chunk, steps = 0, 0

                def done(self, ins):
                    ins.then_inc(s_v, 1)
                    self.steps += 1

                def settle(self):
                    dv.wait_ge(s_v, self.chunk * VSTEPS + self.steps)

            fr = Front()

            def scan(d, g, n, q):
                k = g * ND + d
                if d == 0:
                    dv.wait_ge(s_bcl[q], (g - q) * 16 + 32)
                dv.tensor_tensor(dBu[:, :, :], du[:, d:d + 1, :].to_broadcast([P, NS, TC]), Bb[q][:, :, :],
                                 ALU.mult).then_inc(s_dBu, 1)
                dv.wait_ge(s_dBu, k + 1)
                dv.wait_ge(s_dA, k + 1)
                dv.wait_ge(s_hC, k - 1 + CR)
                for i in range(NS):
                    at = bass.ds(n * NS + (d * N + i), 1)
                    hs = dv.tensor_tensor_scan(h[d % 2][:, i, :], dA[d % 2][:, i, :], dBu[:, i, :],
                                               state[:, at], ALU.mult, ALU.add)
                hs.then_inc(s_h, 1)
                dv.wait_ge(s_h, k + 1 + CR)
                plain(dv)
                dv.tensor_copy(state[:, bass.ds(n * NS + d * N, NS)], h[d % 2][:, :, TC - 1]).then_inc(s_st, 1)

            def scale_w2(slot, w, unit, use):
                dv.wait_ge(s_w[slot], (use + 1) * 32)
                for f in range(NF):
                    m = dv.tensor_scalar(w2[slot][:, f, :], w2[slot][:, f, :], mu[:, bass.ds(unit * NF + f, 1)],
                                         None, ALU.mult)
                m.then_inc(s_w2, 1)

            def product(slot, w, unit):
                for f in range(NF):
                    dv.wait_ge(s_f1, w * 2 * NF + NF + f + 1)
                    dv.wait_ge(s_g, w * NF + f + 1 + HS)
                    a = act[slot][:, f, :]
                    dv.scalar_tensor_tensor(out=a, in0=fh[(2, 0)[f]][:, :], scalar=b1[:, bass.ds(unit * 2 * NF + f, 1)],
                                            in1=a, op0=ALU.add, op1=ALU.mult).then_inc(s_a, 1)

            def add(slot, o, half, unit):
                dv.wait_ge(s_o, o + 1)
                dv.wait_ge(s_oc, o + HS)
                for t in range(2):
                    tt = half * 2 + t
                    row = xa[:, slot, tt, :]
                    by = 1.0 if unit is None else comb[:, bass.ds(unit + tt * (E + 1), 1)]
                    s = dv.scalar_tensor_tensor(out=row, in0=po[:, t * DM:(t + 1) * DM], scalar=by, in1=row,
                                                op0=ALU.mult, op1=ALU.add)
                s.then_inc(s_oc, 1)

            for c, b, cc in chunks(dv):
                fr.chunk, fr.steps = c, 0
                X = xa[:, cc % 2, :, :]
                dv.wait_ge(s_x, (c + 1) * 16)
                for t in range(NT):
                    fr.done(dv.bn_stats(st[:, t, :], X[:, t, :]))
                fr.settle()
                plain(dv)
                for t in range(NT):
                    fr.done(dv.bn_aggr(mv[:, t, :], st[:, t, :]))
                fr.settle()
                dv.tensor_scalar(var[:, :], mv[:, :, 1], 1e-5, None, ALU.add).then_inc(s_var, 1)
                dv.wait_ge(s_sd, c + 1)
                fr.done(dv.reciprocal(rstd[:, :], dev[:, :]))
                fr.settle()
                for t in range(NT):
                    dv.tensor_scalar(xn[:, t, :], X[:, t, :], mv[:, t, 0:1], rstd[:, t:t + 1], ALU.subtract,
                                     ALU.mult).then_inc(s_xn, 1)
                dv.wait_ge(s_lg, c + 1)
                fr.done(dv.tensor_copy(sc[:, :, :], y[2][:, 0:NT * E].rearrange("p (t e) -> p t e", e=E)))
                fr.settle()
                fr.done(dv.tensor_reduce(r4[:, :], sc[:, :, :], AX.X, ALU.max))
                fr.settle()
                dv.tensor_tensor(lg[:, :, :], sc[:, :, :], spread(r4), ALU.subtract).then_inc(s_lsub, 1)
                if cc == 0:
                    dv.memset(xr[:, :, 0:HALO], 0.0).then_inc(s_zero, 1)
                    dv.memset(state[:, :], 0.0).then_inc(s_zero, 1)
                    dv.wait_ge(s_zero, (b + 1) * 2)
                for d in range(ND):
                    dv.wait_ge(s_ipc, c * 2 * ND + d + 1)
                    fr.done(dv.tensor_scalar(cv[:, d, :], xr[:, d, 0:TC], cw[:, d, 0:1], cb[:, d:d + 1],
                                             ALU.mult, ALU.add))
                for k in range(1, TAPS):
                    for d in range(ND):
                        dv.wait_ge(s_v, c * VSTEPS + fr.steps - ND + 1 + (d if k == TAPS - 1 else 0))
                        s = dv.scalar_tensor_tensor(out=cv[:, d, :], in0=xr[:, d, k:k + TC], scalar=cw[:, d, k:k + 1],
                                                    in1=cv[:, d, :], op0=ALU.mult, op1=ALU.add)
                        if k < TAPS - 1:
                            fr.done(s)
                        else:
                            s.then_inc(s_cv, 1)
                dv.wait_ge(s_cv, (c + 1) * ND)
                dv.tensor_copy(xr[:, :, 0:HALO], xr[:, :, TC:TC + HALO]).then_inc(s_halo, 1)
                dv.wait_ge(s_lexp, c + 1)
                fr.done(dv.tensor_reduce(r5[:, :], lg[:, :, :], AX.X, ALU.add))
                fr.settle()
                fr.done(dv.reciprocal(r4[:, :], r5[:, :]))
                fr.settle()
                fr.done(dv.tensor_tensor(sc[:, :, :], lg[:, :, :], spread(r4), ALU.mult))
                fr.settle()
                left = sc
                for k in range(TOPK):
                    fr.done(dv.tensor_reduce(r4[:, :], left[:, :, :], AX.X, ALU.max))
                    fr.settle()
                    fr.done(dv.tensor_tensor(eq[:, :, :], left[:, :, :], spread(r4), ALU.is_equal))
                    fr.settle()
                    fr.done(dv.tensor_tensor(eq[:, :, :], eq[:, :, :], prio[:, :, :], ALU.mult))
                    fr.settle()
                    fr.done(dv.tensor_reduce(r5[:, :], eq[:, :, :], AX.X, ALU.max))
                    fr.settle()
                    fr.done(dv.tensor_tensor(eq[:, :, :], eq[:, :, :], spread(r5), ALU.is_equal))
                    fr.settle()
                    fr.done(dv.scalar_tensor_tensor(out=sm[:, :, :], in0=eq[:, :, :], scalar=-2.0,
                                                    in1=left[:, :, :], op0=ALU.mult, op1=ALU.add))
                    fr.settle()
                    left = sm
                fr.done(dv.scalar_tensor_tensor(out=eq[:, :, :], in0=sm[:, :, :], scalar=0.0, in1=sc[:, :, :],
                                                op0=ALU.is_lt, op1=ALU.mult))
                fr.settle()
                fr.done(dv.tensor_reduce(r4[:, :], eq[:, :, :], AX.X, ALU.add))
                fr.settle()
                fr.done(dv.tensor_scalar(r5[:, :], r4[:, :], 1e-20, None, ALU.add))
                fr.settle()
                fr.done(dv.reciprocal(r4[:, :], r5[:, :]))
                fr.settle()
                dv.tensor_tensor(comb[:, :].rearrange("p (t e) -> p t e", e=E + 1)[:, :, 0:E], eq[:, :, :],
                                 spread(r4), ALU.mult).then_inc(s_comb, 1)
                for d in range(ND):
                    k = c * ND + d
                    s = d % 2
                    ex, lo = spe[:, s, :], spl[:, s, :]
                    dv.wait_ge(s_spl, k + 1)
                    fr.done(dv.tensor_scalar(spm[:, :], ex, 0.02, None, ALU.is_lt))
                    fr.done(dv.tensor_scalar(spq[:, :], ex, -0.25, 1.0 / 3.0, ALU.mult, ALU.add))
                    fr.settle()
                    fr.done(dv.tensor_tensor(spq[:, :], spq[:, :], ex, ALU.mult))
                    fr.settle()
                    for term in (-0.5, 1.0):
                        fr.done(dv.scalar_tensor_tensor(out=spq[:, :], in0=spq[:, :], scalar=term, in1=ex,
                                                        op0=ALU.add, op1=ALU.mult))
                        fr.settle()
                    plain(dv)
                    fr.done(dv.copy_predicated(lo, spm[:, :], spq[:, :]))
                    fr.settle()
                    dv.scalar_tensor_tensor(out=delta[:, d, :], in0=spx[:, s, :], scalar=0.0, in1=lo,
                                            op0=ALU.max, op1=ALU.add).then_inc(s_dl, 1)
                    dv.wait_ge(s_dl, k + 1)
                    dv.tensor_tensor(du[:, d, :], delta[:, d, :], u[:, d, :], ALU.mult).then_inc(s_du, 1)
                assert fr.steps == VSTEPS, fr.steps
                for half in range(2):
                    add(cc % 2, c * OUSE + half, half, None)
                dv.wait_ge(s_du, (c + 1) * ND)
                dv.wait_ge(s_st, c * NG * ND + HS)
                for n, q in groups(dv):
                    g = c * NG + n
                    w = c * UNITS + n * 2
                    o = c * OUSE + 2 + n * 4
                    scale_w2(0, w, n * 2, g)
                    scan(0, g, n, q)
                    scan(1, g, n, q)
                    product(0, w, n * 2)
                    scale_w2(1, w + 1, n * 2 + 1, g)
                    scan(2, g, n, q)
                    product(1, w + 1, n * 2 + 1)
                    add(cc % 2, o, 0, n * 2)
                    add(cc % 2, o + 1, 1, n * 2)
                    scan(3, g, n, q)
                    add(cc % 2, o + 2, 0, n * 2 + 1)
                    add(cc % 2, o + 3, 1, n * 2 + 1)
                w = (c + 1) * UNITS - 1
                o = (c + 1) * OUSE - 4
                dv.wait_ge(s_ns, (c + 1) * NG * ND + CR)
                for d in range(ND):
                    dv.tensor_tensor(cv[:, d, :], sres[:, d, :], y[d][:, :], ALU.mult).then_inc(s_yg, 1)
                scale_w2(2, w, UNITS - 1, c)
                product(2, w, UNITS - 1)
                for k in range(4):
                    add(cc % 2, o + k, k % 2, None)


def kernel(**inputs):
    import numpy as _np
    import concourse.bacc as _bacc
    from concourse import mybir as _mybir
    from concourse.bass_utils import run_bass_kernel_spmd as _run

    a = {k[3:]: _np.asarray(v) for k, v in inputs.items()}
    P = 128
    E = a["ffn_gate_w"].shape[0]
    DM = a["attn_x"].shape[2]
    F = a["ffn_fc2_w"].shape[2]
    FS = a["ffn_s_fc2_w"].shape[1]
    NT = 4

    def parts(m):
        return _np.ascontiguousarray(_np.swapaxes(m.reshape(m.shape[0] // P, P, *m.shape[1:]), 0, 1))

    def half(m, lo, axis=0):
        return _np.take(m, range(lo, lo + F), axis=axis)

    s1, s1b = a["ffn_s_fc1_w"], a["ffn_s_fc1_b"]
    fc1 = [m for m in a["ffn_fc1_w"]]
    fc1_b = [m for m in a["ffn_fc1_b"]]
    mult = [m for m in a["ffn_geglu_mult"]]
    fc2 = [m for m in a["ffn_fc2_w"]]
    for lo in range(0, FS, F):
        fc1.append(_np.concatenate([half(s1, lo), half(s1, FS + lo)]))
        fc1_b.append(_np.concatenate([half(s1b, lo), half(s1b, FS + lo)]))
        mult.append(half(a["ffn_s_geglu_mult"], lo))
        fc2.append(half(a["ffn_s_fc2_w"], lo, 1))

    def columns(vectors):
        v = _np.stack(vectors)
        return _np.ascontiguousarray(v.reshape(-1, P).T)

    data = {
        "x": a["attn_x"], "w_in": parts(a["attn_W_in"]),
        "conv_w": parts(_np.ascontiguousarray(a["attn_conv_w"][:, 0, :].T)), "conv_b": columns([a["attn_conv_b"]]),
        "w_x": parts(a["attn_W_x"]), "w_dt": a["attn_W_dt"], "b_dt": columns([a["attn_b_dt"]]),
        "a_log": parts(a["attn_A_log"]).reshape(P, -1), "d_skip": columns([a["attn_D"]]), "w_out": parts(a["attn_W_out"]),
        "gate_w": parts(_np.ascontiguousarray(a["ffn_gate_w"].T)),
        "fc1": _np.stack([parts(_np.ascontiguousarray(m.T)) for m in fc1]), "fc1_b": columns(fc1_b),
        "mult": columns(mult), "fc2": _np.stack([parts(_np.ascontiguousarray(m.T)) for m in fc2]),
        "fc2_b": _np.concatenate([a["ffn_fc2_b"], a["ffn_s_fc2_b"][None]]),
        "ident": _np.eye(P, dtype=_np.float32),
        "prio": _np.broadcast_to(_np.arange(E, 0, -1, dtype=_np.float32), (P, NT, E)),
    }
    nc = _bacc.Bacc("TRN2", target_bir_lowering=False, num_devices=1)
    arrays, args = {}, []
    for name, v in data.items():
        v = _np.ascontiguousarray(v)
        arrays[f"in_{name}"] = v
        args.append(nc.dram_tensor(f"in_{name}", v.shape, _mybir.dt.from_np(v.dtype), kind="ExternalInput").ap())
    args.append(nc.dram_tensor("out", a["attn_x"].shape, _mybir.dt.float32, kind="ExternalOutput").ap())
    mamba_moe_block(nc, *args)
    r = _run(nc, [arrays], core_ids=[0])
    return r.results[0]["out"]
```

```python
import concourse.bass as bass
from concourse import mybir
from contextlib import ExitStack


def mamba_moe_block(nc, x, w_in, conv_w, conv_b, w_x, w_dt, b_dt, a_log, d_skip, w_out, gate_w,
                    packs, fc2_b, ident_in, tri_in, prio_in, restart_in, tiles_in, out):
    fp32 = mybir.dt.float32
    u32 = mybir.dt.uint32
    ALU = mybir.AluOpType
    ACT = mybir.ActivationFunctionType
    AX = mybir.AxisListType

    P = 128
    B, L, DM = x.shape
    KM = DM // P
    ND = w_out.shape[1]
    DIN = ND * P
    R = w_dt.shape[0]
    N = a_log.shape[1] // ND
    XD = w_x.shape[2]
    TAPS = conv_w.shape[2]
    HALO = TAPS - 1
    TC = 512
    NT = TC // P
    CPB = L // TC
    NC = B * CPB
    TT = NC * NT
    E = gate_w.shape[2]
    TOPK = 3
    NF = 2
    F = NF * P
    W1, W2, B1, MU = 0, KM * 2 * F, KM * 2 * F + NF * DM, KM * 2 * F + NF * DM + 2 * NF
    PACK = MU + NF
    ST = 256
    NST = ST // P
    NS = 2
    NG = N // NS
    SLOT_TILES = NC * NG
    MAXT = B * L // ST
    assert packs.shape[2] == PACK and packs.shape[0] == E + 2 and NG % 2 == 0 and NC % 2 == 0
    assert SLOT_TILES >= (TOPK * B * L + E * (ST - 1)) // ST

    xf = x.rearrange("b (t p) d -> p (b t) d", p=P)
    xc = x.rearrange("b (c t p) d -> (b c) p t d", p=P, t=NT)
    outc = out.rearrange("b (c t p) d -> (b c) p t d", p=P, t=NT)

    def dram(name, shape):
        return nc.dram_tensor(name, shape, fp32, kind="Internal").ap()

    bc_dram = dram("bc_rows", [2, 2, N, TC])
    xnT_dram = dram("xn_transposed", [NC, P, KM * TC])
    part = dram("partial_sums", [NC, P, NT * DM])
    x_slots = dram("slot_inputs", [(SLOT_TILES + 1) * ST, DM])
    y_slots = dram("slot_outputs", [(SLOT_TILES + 1) * ST, DM])
    xsl = x_slots.rearrange("(g t p) d -> g p t d", p=P, t=NST)
    ysl = y_slots.rearrange("(g t p) d -> g p t d", p=P, t=NST)

    ctx = ExitStack()
    with ctx:
        def sb(name, shape, dt=fp32):
            return ctx.enter_context(nc.sbuf_tensor(name, shape, dt))

        def pb(name):
            return ctx.enter_context(nc.psum_tensor(name, [P, 512], fp32))

        def sem(name):
            return ctx.enter_context(nc.semaphore(name))

        ident = sb("ident", [P, P])
        tri = sb("tri", [P, P])
        ones = sb("ones", [P, P])
        prio = sb("prio", [P, TT * E])
        restart = sb("restart", [P, E * TT])
        tiles = sb("tiles", [P, SLOT_TILES])
        win = sb("win", [P, KM, 2 * DIN])
        wx = sb("wx", [P, ND, XD])
        wdt = sb("wdt", [R, DIN])
        wout = sb("wout", [P, ND, DM])
        gw = sb("gw", [P, KM, E])
        cw = sb("cw", [P, ND, TAPS])
        cb = sb("cb", [P, ND])
        bdt = sb("bdt", [P, ND])
        al = sb("al", [P, ND * N])
        am = sb("am", [P, ND * N])
        dsk = sb("dsk", [P, ND])
        dskip = sb("dskip", [P, ND, P])
        b2 = sb("b2", [E + 1, DM])
        zero = sb("zero", [P, DM])
        region = sb("region", [P, TT * DM])
        xall = region
        cv, u, delta, du = (region[:, i * ND * TC:(i + 1) * ND * TC].rearrange("p (d t) -> p d t", d=ND)
                            for i in range(4))
        gy = [region[:, i * TOPK * NT * DM:(i + 1) * TOPK * NT * DM].rearrange("p (k d) -> p k d", d=DM)
              for i in range(2)]
        scanbuf = sb("scanbuf", [P, 7 * NS * TC])
        tables = [scanbuf[:, i * TT * E:(i + 1) * TT * E] for i in range(14)]

        def group(i):
            return scanbuf[:, i * NS * TC:(i + 1) * NS * TC].rearrange("p (n t) -> p n t", n=NS)

        dA, dBu, h, hC = [group(0), group(1)], group(2), [group(3), group(4)], [group(5), group(6)]
        spreadbuf = sb("spreadbuf", [P, 4 * NS * TC])
        stage = [spreadbuf[:, i * NT * DM:(i + 1) * NT * DM].rearrange("p (t d) -> p t d", d=DM) for i in range(2)]
        Bb = [spreadbuf[:, i * NS * TC:(i + 1) * NS * TC].rearrange("p (n t) -> p n t", n=NS) for i in (0, 1)]
        Cb = [spreadbuf[:, i * NS * TC:(i + 1) * NS * TC].rearrange("p (n t) -> p n t", n=NS) for i in (2, 3)]
        st = sb("st", [P, TT * 6])
        mean = sb("mean", [P, TT])
        var = sb("var", [P, TT])
        dev = sb("dev", [P, TT])
        rstd = sb("rstd", [P, TT])
        ra = sb("ra", [P, TT])
        rb = sb("rb", [P, TT])
        top = sb("top", [P, TOPK, TT])
        comb = sb("comb", [P, TT * (E + 1)])
        cnt = sb("cnt", [P, E])
        one_e = sb("one_e", [P, E])
        incl = sb("incl", [P, E])
        base = sb("base", [P, E])
        big = sb("big", [P, SLOT_TILES * E])
        tef = sb("tef", [P, SLOT_TILES])
        te = sb("te", [P, SLOT_TILES], u32)
        slot = sb("slot", [P, NC * TOPK * NT], u32)
        wk = sb("wk", [P, NC * TOPK * NT])
        ix = [sb(f"ix{i}", [P, TOPK * NT], u32) for i in range(2)]
        xa = sb("xa", [P, 2, NT, DM])
        xnT = [sb(f"xnT{i}", [P, KM, TC]) for i in range(2)]
        xr = sb("xr", [P, ND, HALO + TC])
        sres = sb("sres", [P, ND, TC])
        xdb = sb("xdb", [XD, TC])
        spx = sb("spx", [P, 2, TC])
        spe = sb("spe", [P, 2, TC])
        spl = sb("spl", [P, 2, TC])
        spq = sb("spq", [P, TC])
        spm = sb("spm", [P, TC], u32)
        combc = sb("combc", [P, NT, E + 1])
        combT = sb("combT", [E + 1, TC])
        state = sb("state", [P, ND * N])
        wp = [sb(f"wp{i}", [P, PACK]) for i in range(2)]
        w1 = [w[:, W1:W2].rearrange("p (k f) -> p k f", k=KM) for w in wp]
        w2 = [w[:, W2:B1].rearrange("p (k f) -> p k f", k=NF) for w in wp]
        act = [sb(f"act{i}", [P, NF, TC]) for i in range(2)]
        xs = [sb(f"xs{i}", [P, NST, DM]) for i in range(2)]
        xsT = [sb(f"xsT{i}", [P, KM, ST]) for i in range(2)]
        ys = [sb(f"ys{i}", [P, NST, DM]) for i in range(2)]

        y = [pb(f"y{i}") for i in range(4)]
        fh = [pb(f"fh{i}") for i in range(3)]
        po = pb("po")

        s_mark = sem("waits_taken")
        s_const = sem("constants_loaded")
        s_am = sem("decay_exponentiated")
        s_init = sem("constants_set")
        s_made = sem("constants_made")
        s_xq = [sem(f"x_quarter_{i}") for i in range(4)]
        s_v = sem("vector_steps")
        s_bn = sem("row_statistics")
        s_var = sem("variance_ready")
        s_sd = sem("deviation_ready")
        s_xn = sem("xn_ready")
        s_stage = [sem(f"rows_staged_{i}") for i in range(2)]
        s_T = sem("xn_transposed_psum")
        s_xnT = sem("xnT_copied")
        s_xts = [sem(f"xnT_stored_{i}") for i in range(2)]
        s_lsub = sem("logits_shifted")
        s_lexp = sem("logits_exponentiated")
        s_mask = sem("chosen_ready")
        s_rank = sem("ranks_ready")
        s_slot = sem("slots_ready")
        s_zf = sem("slots_zeroed")
        s_st2 = sem("rows_staged_for_slots")
        s_ix = sem("indices_copied")
        s_sc = [sem(f"rows_scattered_{i}") for i in range(2)]
        s_xt = sem("xnT_loaded")
        s_xa = sem("sums_loaded")
        s_xst = sem("sums_stored")
        s_ws = sem("shared_weights_loaded")
        s_ws2 = sem("shared_fc2_scaled")
        s_f1 = sem("shared_fc1_ready")
        s_g = sem("shared_gelu_ready")
        s_a = sem("shared_product_ready")
        s_o = sem("shared_out_ready")
        s_oc = sem("shared_out_added")
        s_zero = sem("batch_zeroed")
        s_lgf = sem("logits_made")
        s_cc = sem("chunk_weights_copied")
        s_ct = sem("weights_transposed")
        s_ctc = sem("weightsT_copied")
        s_ip = sem("inproj_ready")
        s_ipc = sem("inproj_copied")
        s_cv = sem("conv_ready")
        s_halo = sem("halo_kept")
        s_u = sem("u_ready")
        s_xd = sem("xdbl_ready")
        s_xdc = sem("xdbl_copied")
        s_bcd = sem("bc_rows_stored")
        s_bcl = [sem(f"bc_spread_{i}") for i in range(2)]
        s_dt = sem("dt_ready")
        s_spab = sem("softplus_abs")
        s_spe = sem("softplus_exp")
        s_spl = sem("softplus_log")
        s_dl = sem("delta_ready")
        s_du = sem("du_ready")
        s_dA = sem("dA_ready")
        s_dBu = sem("dBu_ready")
        s_h = sem("h_ready")
        s_st = sem("state_kept")
        s_hC = sem("hC_ready")
        s_ns = sem("y_accumulated")
        s_yg = sem("y_gated")
        s_co = sem("chunk_out_ready")
        s_coc = sem("chunk_out_added")
        s_mw = [sem(f"expert_weights_{i}") for i in range(2)]
        s_mx = [sem(f"slot_rows_{i}") for i in range(2)]
        s_mw2 = sem("expert_fc2_scaled")
        s_mT = sem("slot_rows_transposed")
        s_mTc = sem("slot_rowsT_copied")
        s_mf = sem("expert_fc1_ready")
        s_mg = sem("expert_gelu_ready")
        s_ma = sem("expert_product_ready")
        s_m2 = sem("expert_fc2_ready")
        s_my = sem("slot_out_copied")
        s_mys = [sem(f"slot_out_stored_{i}") for i in range(2)]
        s_gy = [sem(f"rows_gathered_{i}") for i in range(2)]
        s_ga = sem("gathered_added")
        s_gv = sem("gathered_steps")

        CR = 2 * ND
        HS = 1
        NCONST = 16 * 16
        INIT = 4
        VFRONT = 4 * 6
        VCONV = ND * (TAPS - 1)

        def ybank(j):
            return y[(3, 0, 1)[j % 3]]

        def by_tile(t):
            return t[:, :].rearrange("p (t e) -> p t e", e=E)

        def over_e(r):
            return r.unsqueeze(2).to_broadcast([P, TT, E])

        def plain(eng):
            eng.sem_inc(s_mark, 1)

        def pairs(eng):
            plain(eng)
            with eng.Fori(0, NC // 2) as i:
                for q in range(2):
                    yield i * 2 + q, q, i

        def chunks(eng):
            plain(eng)
            with eng.Fori(0, B) as b:
                for cc in range(CPB):
                    yield b * CPB + cc, cc, b

        def groups(eng, c):
            plain(eng)
            with eng.Fori(0, NG // 2) as i:
                for q in range(2):
                    yield i * 2 + q, c * NG + i * 2 + q, q, c * (NG // 2) + i

        block = ctx.enter_context(nc.Block())

        @block.sync
        def _(sp):
            for t, src in ((ident, ident_in), (gw, gate_w)):
                sp.dma_start(t[(slice(None),) * len(t.shape)], src[(slice(None),) * len(t.shape)])\
                    .then_inc(s_const, 16)
            for i in range(4):
                sp.dma_start(xall[:, i * 8 * DM:(i + 1) * 8 * DM].rearrange("p (t d) -> p t d", d=DM),
                             xf[:, i * 8:(i + 1) * 8, :]).then_inc(s_xq[i], 16)
            for t, src in ((tri, tri_in), (prio, prio_in), (restart, restart_in), (tiles, tiles_in),
                           (win, w_in), (wx, w_x), (wdt, w_dt), (wout, w_out), (cw, conv_w), (cb, conv_b),
                           (bdt, b_dt), (al, a_log), (dsk, d_skip), (b2, fc2_b)):
                dims = (slice(None),) * len(t.shape)
                sp.dma_start(t[dims], src[dims]).then_inc(s_const, 16)
            for i in range(2):
                sp.dma_start(wp[i][:, :], packs[E + i]).then_inc(s_ws, 16)
            for c, q, turn in pairs(sp):
                sp.wait_ge(s_xn, (c + 1) * NT)
                plain(sp)
                sp.wait_ge(s_T, c - 1 + CR)
                plain(sp)
                sp.dma_start(stage[q], xall[:, bass.ds(c * NT * DM, NT * DM)]
                             .rearrange("p (t d) -> p t d", d=DM)).then_inc(s_stage[q], 16)

            def load_sums(src, c, parity):
                sp.dma_start(xa[:, parity, :, :], src[bass.ds(c, 1)]
                             .rearrange("a p t d -> (a p) t d")).then_inc(s_xa, 16)

            def store_sums(dst, c, parity, stored):
                sp.dma_start(dst[bass.ds(c, 1)].rearrange("a p t d -> (a p) t d"), xa[:, parity, :, :])\
                    .then_inc(s_xst, 16)
                sp.wait_ge(s_xst, stored * 16)
                plain(sp)

            def load_xnT(c, parity):
                sp.dma_start(xnT[parity][:, :, :], xnT_dram[bass.ds(c, 1)]
                             .rearrange("a p (k t) -> (a p) k t", k=KM)).then_inc(s_xt, 16)

            partc = part.rearrange("c p (t d) -> c p t d", d=DM)
            for q in range(2):
                sp.wait_ge(s_xts[q], NC * 8 + HS)
            sp.wait_ge(s_lgf, NC + CR)
            for c, q, turn in pairs(sp):
                load_sums(xc, c, q)
                load_xnT(c, q)
                sp.wait_ge(s_oc, (c + 1) * 4 + HS)
                store_sums(partc, c, q, c + 1)
            for q in range(2):
                sp.wait_ge(s_sc[q], NC * TOPK * NT * 8)
            for c, cc, b in chunks(sp):
                load_sums(partc, c, cc % 2)
                load_xnT(c, cc % 2)
                if cc > 0:
                    sp.wait_ge(s_coc, c * 4 + HS)
                    store_sums(partc, c - 1, 1 - cc % 2, c + NC)
                sp.wait_ge(s_xdc, c + 1)
                sp.dma_start(bc_dram[cc % 2].rearrange("s n t -> (s n) t"), xdb[R:XD, :]).then_inc(s_bcd, 16)
                sp.wait_ge(s_bcd, (c + 1) * 16 + HS)
                for n, g, q, pair in groups(sp, c):
                    sp.wait_ge(s_h, (g - 1) * ND + CR)
                    sp.wait_ge(s_hC, (g - 1) * ND + CR)
                    for k, t in enumerate((Bb, Cb)):
                        sp.dma_start(t[q], bc_dram[cc % 2, k, bass.ds(n * NS, NS), :].partition_broadcast(P))\
                            .then_inc(s_bcl[q], 16)
                    sp.wait_ge(s_m2, g - 1 + CR)
                    plain(sp)
                    e = sp.value_load(te[0:1, bass.ds(g, 1)], min_val=0, max_val=E - 1)
                    sp.dma_start(wp[q][:, :], packs[bass.ds(e, 1)].rearrange("a p w -> (a p) w"))\
                        .then_inc(s_mw[q], 16)
                    sp.dma_start(xs[q][:, :, :], xsl[bass.ds(g + 1, 1)].rearrange("a p t d -> (a p) t d"))\
                        .then_inc(s_mx[q], 16)
                if cc == CPB - 1:
                    sp.wait_ge(s_coc, (c + 1) * 4 + HS)
                    store_sums(partc, c, cc % 2, c + 1 + NC)
            for c, q, turn in pairs(sp):
                load_sums(partc, c, q)
                sp.wait_ge(s_ga, c + 1 + CR)
                plain(sp)
                store_sums(outc, c, q, c + 1 + 2 * NC)

        @block.tensor
        def _(pe):
            pe.wait_ge(s_const, NCONST)
            pe.wait_ge(s_init, INIT)
            for c, q, turn in pairs(pe):
                pe.wait_ge(s_stage[q], (turn + 1) * 16)
                pe.wait_ge(s_xnT, (c - 1) * KM + CR)
                for t in range(NT):
                    for m in range(KM):
                        mm = pe.transpose(y[2 * q + m][:, t * P:(t + 1) * P], stage[q][:, t, m * P:(m + 1) * P],
                                          ident[:, :])
                mm.then_inc(s_T, 1)
                pe.wait_ge(s_xnT, (c + 1) * KM + CR)
                for t in range(NT):
                    for m in range(KM):
                        mm = pe.matmul(po[:, bass.ds(c * (NT * E) + t * E, E)], xnT[q][:, m, t * P:(t + 1) * P],
                                       gw[:, m, :], start=(m == 0), stop=(m == KM - 1))
                mm.then_inc(s_lgf, 1)
            pe.wait_ge(s_mask, 1)
            pe.matmul(y[0][:, 0:TT * E], tri[:, :], tables[3], start=True, stop=True).then_inc(s_rank, 1)
            pe.matmul(y[1][:, 0:TT * E], ones[:, :], tables[3], start=True, stop=True).then_inc(s_rank, 1)

            pe.wait_ge(s_ws2, 2)
            for c, q, turn in pairs(pe):
                for i in range(2):
                    w = c * 2 + i
                    if i == 0:
                        pe.wait_ge(s_xt, (c + 1) * 16)
                    pe.wait_ge(s_g, w * NF + HS)
                    pe.wait_ge(s_a, w * NF + HS)
                    for k, ft in enumerate((NF, NF + 1, 0, 1)):
                        if k == 3:
                            pe.wait_ge(s_g, w * NF + 1 + HS)
                        for m in range(KM):
                            mm = pe.matmul(fh[k % 3][:, :], w1[i][:, m, ft * P:(ft + 1) * P], xnT[q][:, m, :],
                                           start=(m == 0), stop=(m == KM - 1))
                        mm.then_inc(s_f1, 1)
                for i in range(2):
                    pe.wait_ge(s_a, (c * 2 + i + 1) * NF + HS)
                    for half in range(2):
                        pe.wait_ge(s_oc, c * 4 + i * 2 + half + HS)
                        for t in range(2):
                            tok = (half * 2 + t) * P
                            for f in range(NF):
                                mm = pe.matmul(po[:, t * DM:(t + 1) * DM], act[i][:, f, tok:tok + P], w2[i][:, f, :],
                                               start=(f == 0), stop=(f == NF - 1))
                        mm.then_inc(s_o, 1)

            def state_sum(d, k):
                pe.wait_ge(s_hC, k + 1 + CR)
                for i in range(NS):
                    mm = pe.matmul(y[d][:, :], ident[:, :], hC[d % 2][:, i, :], start=False, stop=False,
                                   skip_group_check=True)
                mm.then_inc(s_ns, 1)

            pe.wait_ge(s_made, 1 + ND)
            for c, cc, b in chunks(pe):
                pe.wait_ge(s_yg, c * ND + HS)
                pe.wait_ge(s_xt, (c + 1 + NC) * 16)
                for j in range(2 * ND):
                    if j >= 3:
                        pe.wait_ge(s_ipc, c * 2 * ND + j - 2)
                    for m in range(KM):
                        mm = pe.matmul(ybank(j)[:, :], win[:, m, j * P:(j + 1) * P], xnT[cc % 2][:, m, :],
                                       start=(m == 0), stop=(m == KM - 1))
                    mm.then_inc(s_ip, 1)
                pe.wait_ge(s_cc, c + 1)
                for t in range(NT):
                    mm = pe.transpose(y[2][0:E + 1, t * P:(t + 1) * P], combc[:, t, :], ident[:, :])
                mm.then_inc(s_ct, 1)
                pe.wait_ge(s_ctc, c + 1 + HS)
                pe.wait_ge(s_coc, c * 4 + HS)
                for half in range(2):
                    for t in range(2):
                        tok = (half * 2 + t) * P
                        mm = pe.matmul(fh[1 + half][:, t * DM:(t + 1) * DM], combT[:, tok:tok + P], b2[:, :],
                                       start=True, stop=True)
                    mm.then_inc(s_co, 1)
                pe.wait_ge(s_ipc, (c + 1) * 2 * ND)
                for d in range(ND):
                    pe.wait_ge(s_u, c * ND + d + 1)
                    mm = pe.matmul(y[1][0:XD, :], wx[:, d, :], u[:, d, :], start=(d == 0), stop=(d == ND - 1))
                mm.then_inc(s_xd, 1)
                pe.wait_ge(s_xdc, c + 1)
                for d in range(ND):
                    if d >= 2:
                        pe.wait_ge(s_spab, c * ND + d - 1)
                    pe.matmul(y[(0, 3)[d % 2]][:, :], wdt[:, d * P:(d + 1) * P], xdb[0:R, :],
                              start=True, stop=True).then_inc(s_dt, 1)
                pe.wait_ge(s_spab, (c + 1) * ND)
                for d in range(ND):
                    pe.matmul(y[d][:, :], dskip[:, d, :], u[:, d, :], start=True, stop=False,
                              skip_group_check=True)
                pe.wait_ge(s_coc, c * 4 + 2 + HS)
                for n, g, q, pair in groups(pe, c):
                    k = g * ND
                    pe.wait_ge(s_mx[q], (pair + 1) * 16)
                    for t in range(NST):
                        for m in range(KM):
                            mm = pe.transpose(fh[0][:, m * ST + t * P:m * ST + (t + 1) * P],
                                              xs[q][:, t, m * P:(m + 1) * P], ident[:, :])
                    mm.then_inc(s_mT, 1)
                    state_sum(0, k)
                    state_sum(1, k + 1)
                    pe.wait_ge(s_mTc, g + 1)
                    pe.wait_ge(s_mw[q], (pair + 1) * 16)
                    for bank, first in ((1, NF), (2, 0)):
                        for f in range(NF):
                            ft = first + f
                            for m in range(KM):
                                mm = pe.matmul(fh[bank][:, f * ST:(f + 1) * ST], w1[q][:, m, ft * P:(ft + 1) * P],
                                               xsT[q][:, m, :], start=(m == 0), stop=(m == KM - 1))
                        mm.then_inc(s_mf, 1)
                    state_sum(2, k + 2)
                    state_sum(3, k + 3)
                    pe.wait_ge(s_ma, g + 1)
                    pe.wait_ge(s_mw2, g + 1)
                    pe.wait_ge(s_my, g + 1)
                    for t in range(NST):
                        for f in range(NF):
                            mm = pe.matmul(po[:, t * DM:(t + 1) * DM], act[q][:, f, t * P:(t + 1) * P], w2[q][:, f, :],
                                           start=(f == 0), stop=(f == NF - 1))
                    mm.then_inc(s_m2, 1)
                pe.wait_ge(s_yg, (c + 1) * ND + HS)
                for half in range(2):
                    for t in range(2):
                        tok = (half * 2 + t) * P
                        for d in range(ND):
                            mm = pe.matmul(fh[1 + half][:, t * DM:(t + 1) * DM], cv[:, d, tok:tok + P], wout[:, d, :],
                                           start=(d == 0), stop=(d == ND - 1))
                    mm.then_inc(s_co, 1)

        @block.scalar
        def _(sa):
            sa.wait_ge(s_init, INIT)
            rows = (SLOT_TILES + 1) * ST // P
            sa.dma_start(x_slots.rearrange("(p r) d -> p r d", p=P),
                         zero[:, :].unsqueeze(1).to_broadcast([P, rows, DM])).then_inc(s_zf, 16)
            sa.wait_ge(s_const, NCONST)
            sa.activation(am[:, :], al[:, :], ACT.Exp).then_inc(s_am, 1)
            sa.wait_ge(s_var, 1)
            sa.activation(dev[:, :], var[:, :], ACT.Sqrt).then_inc(s_sd, 1)
            for c, q, turn in pairs(sa):
                sa.wait_ge(s_T, c + 1 + CR)
                sa.wait_ge(s_lgf, c - 1 + CR)
                sa.wait_ge(s_xts[q], turn * 16 + HS)
                for m in range(KM):
                    sa.activation(xnT[q][:, m, :], y[2 * q + m][:, :], ACT.Copy).then_inc(s_xnT, 1)
                sa.wait_ge(s_xnT, (c + 1) * KM + CR)
                sa.dma_start(xnT_dram[bass.ds(c, 1)].rearrange("a p (k t) -> (a p) k t", k=KM), xnT[q][:, :, :])\
                    .then_inc(s_xts[q], 16)
            sa.wait_ge(s_lsub, 1)
            sa.activation(tables[1], tables[1], ACT.Exp).then_inc(s_lexp, 1)

            for c, q, turn in pairs(sa):
                for i in range(2):
                    w = c * 2 + i
                    sa.wait_ge(s_oc, c * 4 + HS)
                    for f in range(NF):
                        sa.wait_ge(s_f1, w * 2 * NF + f + 1)
                        sa.activation(act[i][:, f, :], fh[f][:, :], ACT.Gelu,
                                      bias=wp[i][:, B1 + NF + f:B1 + NF + f + 1]).then_inc(s_g, 1)

            sa.wait_ge(s_made, 1 + ND)
            for c, cc, b in chunks(sa):
                sa.wait_ge(s_halo, c + HS)
                for j in range(ND):
                    sa.wait_ge(s_ip, c * 2 * ND + j + 1)
                    sa.activation(xr[:, j, HALO:], ybank(j)[:, :], ACT.Copy).then_inc(s_ipc, 1)
                for j in range(ND, 2 * ND):
                    sa.wait_ge(s_ip, c * 2 * ND + j + 1)
                    sa.activation(sres[:, j - ND, :], ybank(j)[:, :], ACT.Silu).then_inc(s_ipc, 1)
                sa.wait_ge(s_ct, c + 1)
                sa.activation(combT[:, :], y[2][0:E + 1, :], ACT.Copy).then_inc(s_ctc, 1)
                for d in range(ND):
                    sa.wait_ge(s_cv, c * ND + d + 1)
                    sa.activation(u[:, d, :], cv[:, d, :], ACT.Silu).then_inc(s_u, 1)
                sa.wait_ge(s_xd, c + 1)
                sa.wait_ge(s_bcd, c * 16 + HS)
                sa.activation(xdb[:, :], y[1][0:XD, :], ACT.Copy).then_inc(s_xdc, 1)
                for d in range(ND):
                    k = c * ND + d
                    bank = y[(0, 3)[d % 2]]
                    sa.wait_ge(s_dt, k + 1)
                    if d >= 2:
                        sa.wait_ge(s_dl, k - 1)
                    sa.activation(spx[:, d % 2, :], bank[:, :], ACT.Identity, bias=bdt[:, d:d + 1])
                    sa.activation(spe[:, d % 2, :], bank[:, :], ACT.Abs, bias=bdt[:, d:d + 1]).then_inc(s_spab, 1)
                    sa.wait_ge(s_spab, k + 1)
                    sa.activation(spe[:, d % 2, :], spe[:, d % 2, :], ACT.Exp, scale=-1.0).then_inc(s_spe, 1)
                    sa.wait_ge(s_spe, k + 1)
                    sa.activation(spl[:, d % 2, :], spe[:, d % 2, :], ACT.Ln, bias=1.0).then_inc(s_spl, 1)
                sa.wait_ge(s_dl, (c + 1) * ND)

                def decay(d, g, n):
                    sa.wait_ge(s_h, g * ND + d - 1 + CR)
                    for i in range(NS):
                        e = sa.activation(dA[d % 2][:, i, :], delta[:, d, :], ACT.Exp,
                                          scale=am[:, bass.ds(n * NS + (d * N + i), 1)])
                    e.then_inc(s_dA, 1)

                def store_slots(g, q, turn):
                    sa.wait_ge(s_m2, g + CR)
                    sa.wait_ge(s_mys[q], turn * 16 + HS)
                    sa.activation(ys[q][:, :, :], po[:, :].rearrange("p (t d) -> p t d", d=DM), ACT.Copy)\
                        .then_inc(s_my, 1)
                    sa.wait_ge(s_my, g + 1)
                    sa.dma_start(ysl[bass.ds(g, 1)].rearrange("a p t d -> (a p) t d"), ys[q][:, :, :])\
                        .then_inc(s_mys[q], 16)

                for n, g, q, pair in groups(sa, c):
                    sa.wait_ge(s_mT, g + 1)
                    sa.activation(xsT[q][:, :, :], fh[0][:, :].rearrange("p (k s) -> p k s", k=KM), ACT.Copy)\
                        .then_inc(s_mTc, 1)
                    decay(0, g, n)
                    decay(1, g, n)
                    store_slots(g, q, pair)
                    decay(2, g, n)
                    decay(3, g, n)
                    sa.wait_ge(s_mf, g * 2 + 1)
                    for f in range(NF):
                        e = sa.activation(act[q][:, f, 0:ST], fh[1][:, f * ST:(f + 1) * ST], ACT.Gelu,
                                          bias=wp[q][:, B1 + NF + f:B1 + NF + f + 1])
                    e.then_inc(s_mg, 1)
            store_slots(SLOT_TILES, 0, SLOT_TILES // 2)

        @block.gpsimd
        def _(gp):
            gp.memset(zero[:, :], 0.0).then_inc(s_init, 1)
            gp.memset(ones[:, :], 1.0).then_inc(s_init, 1)
            gp.memset(one_e[:, :], 1.0).then_inc(s_init, 1)
            gp.memset(comb[:, :], 1.0).then_inc(s_init, 1)
            for q in (s_T, s_xnT, s_lgf, s_ga, s_h, s_hC, s_ns, s_m2):
                gp.sem_inc(q, CR)
            for q in (s_g, s_a, s_oc, s_yg, s_halo, s_bcd, s_st, s_coc, s_ctc):
                gp.sem_inc(q, HS)
            for q in (*s_xts, *s_mys):
                gp.sem_inc(q, HS)

            def indices(c, q, use):
                gp.tensor_copy(ix[q][:, :], slot[:, bass.ds(c * (TOPK * NT), TOPK * NT)]).then_inc(s_ix, 1)
                gp.wait_ge(s_ix, use + 1)

            gp.wait_ge(s_slot, 2)
            gp.wait_ge(s_zf, 16)
            gp.wait_ge(s_T, NC + CR)
            for c, q, turn in pairs(gp):
                gp.dma_start(stage[q], xall[:, bass.ds(c * NT * DM, NT * DM)]
                             .rearrange("p (t d) -> p t d", d=DM)).then_inc(s_st2, 16)
                plain(gp)
                indices(c, q, c)
                gp.wait_ge(s_st2, (c + 1) * 16)
                plain(gp)
                for j in range(TOPK * NT):
                    gp.indirect_dma_start(x_slots[:, :], bass.IndirectOffsetOnAxis(ix[q][:, j:j + 1], 0),
                                          stage[q][:, j % NT, :], None).then_inc(s_sc[q], 16)
                if q:
                    for k in range(2):
                        gp.wait_ge(s_sc[k], (turn + 1) * (TOPK * NT * 16))
                    plain(gp)
            for c, cc, b in chunks(gp):
                for n, g, q, pair in groups(gp, c):
                    gp.wait_ge(s_bcl[q], (pair + 1) * 32)
                    for d in range(ND):
                        k = g * ND + d
                        gp.wait_ge(s_h, k + 1 + CR)
                        gp.wait_ge(s_ns, k - 1 + CR)
                        gp.tensor_tensor(hC[d % 2], h[d % 2], Cb[q], ALU.mult).then_inc(s_hC, 1)
            gp.wait_ge(s_mys[0], (SLOT_TILES // 2 + 1) * 16 + HS)
            gp.wait_ge(s_mys[1], SLOT_TILES // 2 * 16 + HS)
            gp.wait_ge(s_coc, NC * 4 + HS)
            for c, q, turn in pairs(gp):
                gp.wait_ge(s_ga, c - 1 + CR)
                plain(gp)
                indices(c, q, c + NC)
                plain(gp)
                for j in range(TOPK * NT):
                    gp.indirect_dma_start(gy[q][:, j, :], None, y_slots[:, :],
                                          bass.IndirectOffsetOnAxis(ix[q][:, j:j + 1], 0)).then_inc(s_gy[q], 16)

        @block.vector
        def _(dv):
            class Steps:
                before, steps = 0, 0

                def done(self, ins):
                    ins.then_inc(s_v, 1)
                    self.steps += 1

                def settle(self):
                    dv.wait_ge(s_v, self.before + self.steps)

                def chain(self, ins):
                    self.done(ins)
                    self.settle()

            fr = Steps()
            for i in range(4):
                dv.wait_ge(s_xq[i], 16)
                plain(dv)
                with dv.Fori(0, TT // 4) as t:
                    j = t + i * (TT // 4)
                    dv.bn_stats(st[:, bass.ds(j * 6, 6)], xall[:, bass.ds(j * DM, DM)]).then_inc(s_bn, 1)
            dv.wait_ge(s_bn, TT)
            s6 = st[:, :].rearrange("p (t k) -> p t k", k=6)
            m_even, v_even, m_odd, v_odd = (s6[:, :, k] for k in (1, 2, 4, 5))
            fr.chain(dv.tensor_tensor(ra[:, :], m_even, m_odd, ALU.subtract))
            fr.chain(dv.tensor_tensor(rb[:, :], ra[:, :], ra[:, :], ALU.mult))
            fr.chain(dv.tensor_scalar(rb[:, :], rb[:, :], 0.25, 1e-5, ALU.mult, ALU.add))
            fr.chain(dv.tensor_tensor(ra[:, :], v_even, v_odd, ALU.add))
            dv.scalar_tensor_tensor(out=var[:, :], in0=ra[:, :], scalar=1.0 / DM, in1=rb[:, :], op0=ALU.mult,
                                    op1=ALU.add).then_inc(s_var, 1)
            fr.chain(dv.tensor_tensor(mean[:, :], m_even, m_odd, ALU.add))
            fr.chain(dv.tensor_scalar(mean[:, :], mean[:, :], 0.5, None, ALU.mult))
            dv.wait_ge(s_sd, 1)
            fr.chain(dv.reciprocal(rstd[:, :], dev[:, :]))
            plain(dv)
            with dv.Fori(0, TT) as j:
                row = xall[:, bass.ds(j * DM, DM)]
                dv.tensor_scalar(row, row, mean[:, bass.ds(j, 1)], rstd[:, bass.ds(j, 1)], ALU.subtract,
                                 ALU.mult).then_inc(s_xn, 1)
            dv.wait_ge(s_const, NCONST)
            dv.wait_ge(s_am, 1)
            dv.tensor_scalar(am[:, :], am[:, :], -1.0, None, ALU.mult).then_inc(s_made, 1)
            for d in range(ND):
                dv.tensor_scalar(dskip[:, d, :], ident[:, :], dsk[:, d:d + 1], None, ALU.mult).then_inc(s_made, 1)

            sc, lg, sm, mask = (by_tile(tables[i]) for i in range(4))
            oh = [by_tile(tables[4 + k]) for k in range(TOPK)]
            eq, tot, inc, exc, pos = (tables[7 + i] for i in range(5))
            pr = by_tile(prio)
            dv.wait_ge(s_lgf, NC + CR)
            fr.chain(dv.tensor_copy(tables[0], po[:, 0:TT * E]))
            fr.chain(dv.tensor_reduce(ra[:, :], sc, AX.X, ALU.max))
            dv.tensor_tensor(lg, sc, over_e(ra[:, :]), ALU.subtract).then_inc(s_lsub, 1)
            dv.wait_ge(s_lexp, 1)
            fr.chain(dv.tensor_reduce(ra[:, :], lg, AX.X, ALU.add))
            fr.chain(dv.reciprocal(rb[:, :], ra[:, :]))
            fr.chain(dv.tensor_tensor(sc, lg, over_e(rb[:, :]), ALU.mult))
            left = sc
            for k in range(TOPK):
                fr.chain(dv.tensor_reduce(top[:, k, :], left, AX.X, ALU.max))
                fr.chain(dv.tensor_tensor(by_tile(eq), left, over_e(top[:, k, :]), ALU.is_equal))
                fr.chain(dv.tensor_tensor(by_tile(eq), by_tile(eq), pr, ALU.mult))
                fr.chain(dv.tensor_reduce(rb[:, :], by_tile(eq), AX.X, ALU.max))
                fr.chain(dv.tensor_tensor(oh[k], by_tile(eq), over_e(rb[:, :]), ALU.is_equal))
                fr.chain(dv.scalar_tensor_tensor(out=tables[2], in0=tables[4 + k], scalar=-2.0,
                                                 in1=tables[2] if k else tables[0], op0=ALU.mult, op1=ALU.add))
                left = sm
            dv.tensor_scalar(tables[3], tables[2], 0.0, None, ALU.is_lt).then_inc(s_mask, 1)
            fr.chain(dv.tensor_tensor(ra[:, :], top[:, 0, :], top[:, 1, :], ALU.add))
            fr.chain(dv.tensor_tensor(ra[:, :], ra[:, :], top[:, 2, :], ALU.add))
            fr.chain(dv.tensor_scalar(ra[:, :], ra[:, :], 1e-20, None, ALU.add))
            fr.chain(dv.reciprocal(rb[:, :], ra[:, :]))
            wk4 = wk[:, :].rearrange("p (c k t) -> p k c t", k=TOPK, t=NT)
            for k in range(TOPK):
                fr.done(dv.tensor_tensor(wk4[:, k], top[:, k, :].rearrange("p (c t) -> p c t", t=NT),
                                         rb[:, :].rearrange("p (c t) -> p c t", t=NT), ALU.mult))
            fr.chain(dv.tensor_tensor(by_tile(eq), sc, mask, ALU.mult))
            fr.chain(dv.tensor_tensor(comb[:, :].rearrange("p (t e) -> p t e", e=E + 1)[:, :, 0:E], by_tile(eq),
                                      over_e(rb[:, :]), ALU.mult))
            dv.wait_ge(s_rank, 2)
            by_e = "p (t e) -> p e t"
            fr.chain(dv.tensor_copy(tot.rearrange("p (e t) -> p e t", e=E), y[1][:, 0:TT * E].rearrange(by_e, e=E)))
            fr.chain(dv.tensor_tensor_scan(inc, restart[:, :], tot, 0.0, ALU.mult, ALU.add))
            fr.chain(dv.tensor_tensor(exc, inc, tot, ALU.subtract))
            n_e = inc.rearrange("p (e t) -> p e t", e=E)[:, :, TT - 1:TT]
            fr.chain(dv.tensor_scalar(tef[:, 0:MAXT], tiles[:, 0:MAXT], float(ST), None, ALU.mult))
            cmp = big[:, 0:E * MAXT].rearrange("p (e m) -> p e m", e=E)
            fr.chain(dv.tensor_tensor(cmp, n_e.to_broadcast([P, E, MAXT]),
                                      tef[:, 0:MAXT].unsqueeze(1).to_broadcast([P, E, MAXT]), ALU.is_gt))
            fr.chain(dv.tensor_reduce(cnt[:, :], cmp, AX.X, ALU.add))
            fr.chain(dv.tensor_tensor_scan(incl[:, :], one_e[:, :], cnt[:, :], 0.0, ALU.mult, ALU.add))
            fr.chain(dv.tensor_tensor(base[:, :], incl[:, :], cnt[:, :], ALU.subtract))
            fr.chain(dv.tensor_scalar(base[:, :], base[:, :], 1.0, float(ST), ALU.add, ALU.mult))
            fr.chain(dv.tensor_tensor(exc.rearrange("p (e t) -> p e t", e=E), exc.rearrange("p (e t) -> p e t", e=E),
                                      base[:, :].unsqueeze(2).to_broadcast([P, E, TT]), ALU.add))
            fr.chain(dv.tensor_tensor(by_tile(pos), exc.rearrange("p (e t) -> p t e", e=E),
                                      y[0][:, 0:TT * E].rearrange("p (t e) -> p t e", e=E), ALU.add))
            slot4 = slot[:, :].rearrange("p (c k t) -> p k c t", k=TOPK, t=NT)
            for k in range(TOPK):
                fr.chain(dv.tensor_tensor(by_tile(eq), by_tile(pos), oh[k], ALU.mult))
                fr.chain(dv.tensor_reduce(ra[:, :], by_tile(eq), AX.X, ALU.add))
                fr.chain(dv.tensor_copy(slot4[:, k], ra[:, :].rearrange("p (c t) -> p c t", t=NT)))
            dv.sem_inc(s_slot, 1)
            big3 = big[:, :].rearrange("p (g e) -> p g e", e=E)
            fr.chain(dv.tensor_tensor(big3, tiles[:, :].unsqueeze(2).to_broadcast([P, SLOT_TILES, E]),
                                      incl[:, :].unsqueeze(1).to_broadcast([P, SLOT_TILES, E]), ALU.is_ge))
            fr.chain(dv.tensor_reduce(tef[:, :], big3, AX.X, ALU.add))
            dv.tensor_scalar(te[:, :], tef[:, :], float(E - 1), None, ALU.min).then_inc(s_slot, 1)

            def scale_w2(i, inc_sem):
                for f in range(NF):
                    m = dv.tensor_scalar(w2[i][:, f, :], w2[i][:, f, :], wp[i][:, MU + f:MU + f + 1], None, ALU.mult)
                m.then_inc(inc_sem, 1)

            dv.wait_ge(s_ws, 32)
            for i in range(2):
                scale_w2(i, s_ws2)
            for c, q, turn in pairs(dv):
                for i in range(2):
                    for f in range(NF):
                        w = c * 2 + i
                        dv.wait_ge(s_f1, w * 2 * NF + NF + f + 1)
                        dv.wait_ge(s_g, w * NF + f + 1 + HS)
                        a = act[i][:, f, :]
                        dv.scalar_tensor_tensor(out=a, in0=fh[(2, 0)[f]][:, :], scalar=wp[i][:, B1 + f:B1 + f + 1],
                                                in1=a, op0=ALU.add, op1=ALU.mult).then_inc(s_a, 1)
                dv.wait_ge(s_xa, (c + 1) * 16)
                for k in range(4):
                    dv.wait_ge(s_o, c * 4 + k + 1)
                    dv.wait_ge(s_oc, c * 4 + k + HS)
                    half = k % 2
                    rows = xa[:, q, 2 * half:2 * half + 2, :]
                    dv.tensor_tensor(rows, rows, po[:, :].rearrange("p (t d) -> p t d", d=DM), ALU.add)\
                        .then_inc(s_oc, 1)

            def scan(d, g, n, q, pair):
                k = g * ND + d
                if d == 0:
                    dv.wait_ge(s_bcl[q], (pair + 1) * 32)
                dv.tensor_tensor(dBu, du[:, d:d + 1, :].to_broadcast([P, NS, TC]), Bb[q], ALU.mult)\
                    .then_inc(s_dBu, 1)
                dv.wait_ge(s_dBu, k + 1)
                dv.wait_ge(s_dA, k + 1)
                dv.wait_ge(s_hC, k - 1 + CR)
                for i in range(NS):
                    at = bass.ds(n * NS + (d * N + i), 1)
                    hs = dv.tensor_tensor_scan(h[d % 2][:, i, :], dA[d % 2][:, i, :], dBu[:, i, :],
                                               state[:, at], ALU.mult, ALU.add)
                hs.then_inc(s_h, 1)
                dv.wait_ge(s_h, k + 1 + CR)
                plain(dv)
                dv.tensor_copy(state[:, bass.ds(n * NS + d * N, NS)], h[d % 2][:, :, TC - 1]).then_inc(s_st, 1)

            def add_out(c, cc, k):
                dv.wait_ge(s_co, c * 4 + k + 1)
                dv.wait_ge(s_coc, c * 4 + k + HS)
                half = k % 2
                rows = xa[:, cc % 2, 2 * half:2 * half + 2, :]
                dv.tensor_tensor(rows, rows, fh[1 + half][:, :].rearrange("p (t d) -> p t d", d=DM), ALU.add)\
                    .then_inc(s_coc, 1)

            before = fr.steps
            for q in range(2):
                dv.wait_ge(s_sc[q], NC * TOPK * NT * 8)
            for c, cc, b in chunks(dv):
                fr.before, fr.steps = before + c * (VFRONT + VCONV), 0
                dv.wait_ge(s_ctc, c + HS)
                plain(dv)
                dv.tensor_copy(combc[:, :, :], comb[:, bass.ds(c * (NT * (E + 1)), NT * (E + 1))]
                               .rearrange("p (t e) -> p t e", e=E + 1)).then_inc(s_cc, 1)
                if cc == 0:
                    dv.memset(xr[:, :, 0:HALO], 0.0).then_inc(s_zero, 1)
                    dv.memset(state[:, :], 0.0).then_inc(s_zero, 1)
                    dv.wait_ge(s_zero, (b + 1) * 2)
                for d in range(ND):
                    dv.wait_ge(s_ipc, c * 2 * ND + d + 1)
                    fr.done(dv.tensor_scalar(cv[:, d, :], xr[:, d, 0:TC], cw[:, d, 0:1], cb[:, d:d + 1],
                                             ALU.mult, ALU.add))
                for k in range(1, TAPS):
                    for d in range(ND):
                        dv.wait_ge(s_v, fr.before + fr.steps - ND + 1 + (d if k == TAPS - 1 else 0))
                        s = dv.scalar_tensor_tensor(out=cv[:, d, :], in0=xr[:, d, k:k + TC], scalar=cw[:, d, k:k + 1],
                                                    in1=cv[:, d, :], op0=ALU.mult, op1=ALU.add)
                        if k < TAPS - 1:
                            fr.done(s)
                        else:
                            s.then_inc(s_cv, 1)
                dv.wait_ge(s_cv, (c + 1) * ND)
                dv.tensor_copy(xr[:, :, 0:HALO], xr[:, :, TC:TC + HALO]).then_inc(s_halo, 1)
                dv.wait_ge(s_xa, (c + 1 + NC) * 16)
                for k in range(2):
                    add_out(c, cc, k)
                for d in range(ND):
                    k = c * ND + d
                    s = d % 2
                    ex, lo = spe[:, s, :], spl[:, s, :]
                    dv.wait_ge(s_spl, k + 1)
                    fr.done(dv.tensor_scalar(spm[:, :], ex, 0.02, None, ALU.is_lt))
                    fr.chain(dv.tensor_scalar(spq[:, :], ex, -0.25, 1.0 / 3.0, ALU.mult, ALU.add))
                    fr.chain(dv.tensor_tensor(spq[:, :], spq[:, :], ex, ALU.mult))
                    for term in (-0.5, 1.0):
                        fr.chain(dv.scalar_tensor_tensor(out=spq[:, :], in0=spq[:, :], scalar=term, in1=ex,
                                                         op0=ALU.add, op1=ALU.mult))
                    plain(dv)
                    fr.chain(dv.copy_predicated(lo, spm[:, :], spq[:, :]))
                    dv.scalar_tensor_tensor(out=delta[:, d, :], in0=spx[:, s, :], scalar=0.0, in1=lo,
                                            op0=ALU.max, op1=ALU.add).then_inc(s_dl, 1)
                    dv.wait_ge(s_dl, k + 1)
                    dv.tensor_tensor(du[:, d, :], delta[:, d, :], u[:, d, :], ALU.mult).then_inc(s_du, 1)
                assert fr.steps == VFRONT + VCONV, fr.steps
                dv.wait_ge(s_du, (c + 1) * ND)
                dv.wait_ge(s_st, c * NG * ND + HS)
                for n, g, q, pair in groups(dv, c):
                    dv.wait_ge(s_mw[q], (pair + 1) * 16)
                    scale_w2(q, s_mw2)
                    for d in range(ND):
                        scan(d, g, n, q, pair)
                    dv.wait_ge(s_mf, (g + 1) * 2)
                    dv.wait_ge(s_mg, g + 1)
                    for f in range(NF):
                        a = act[q][:, f, 0:ST]
                        m = dv.scalar_tensor_tensor(out=a, in0=fh[2][:, f * ST:(f + 1) * ST],
                                                    scalar=wp[q][:, B1 + f:B1 + f + 1], in1=a, op0=ALU.add,
                                                    op1=ALU.mult)
                    m.then_inc(s_ma, 1)
                dv.wait_ge(s_ns, (c + 1) * NG * ND + CR)
                for d in range(ND):
                    dv.tensor_tensor(cv[:, d, :], sres[:, d, :], y[d][:, :], ALU.mult).then_inc(s_yg, 1)
                for k in range(2, 4):
                    add_out(c, cc, k)
            for c, q, turn in pairs(dv):
                dv.wait_ge(s_xa, (c + 1 + 2 * NC) * 16)
                dv.wait_ge(s_gy[q], (turn + 1) * (TOPK * NT * 16))
                for k in range(TOPK):
                    if k:
                        dv.wait_ge(s_gv, c * ((TOPK - 1) * NT) + k * NT)
                    for t in range(NT):
                        row = xa[:, q, t, :]
                        m = dv.scalar_tensor_tensor(out=row, in0=gy[q][:, k * NT + t, :],
                                                    scalar=wk[:, bass.ds(c * (TOPK * NT) + k * NT + t, 1)], in1=row,
                                                    op0=ALU.mult, op1=ALU.add)
                        if k < TOPK - 1:
                            m.then_inc(s_gv, 1)
                        elif t == NT - 1:
                            m.then_inc(s_ga, 1)


def kernel(**inputs):
    import numpy as _np
    import concourse.bacc as _bacc
    from concourse import mybir as _mybir
    from concourse.bass_utils import run_bass_kernel_spmd as _run

    a = {k[3:]: _np.asarray(v) for k, v in inputs.items()}
    P = 128
    E = a["ffn_gate_w"].shape[0]
    DM = a["attn_x"].shape[2]
    F = a["ffn_fc2_w"].shape[2]
    FS = a["ffn_s_fc2_w"].shape[1]

    def parts(m):
        return _np.ascontiguousarray(_np.swapaxes(m.reshape(m.shape[0] // P, P, *m.shape[1:]), 0, 1))

    def half(m, lo, axis=0):
        return _np.take(m, range(lo, lo + F), axis=axis)

    s1, s1b = a["ffn_s_fc1_w"], a["ffn_s_fc1_b"]
    fc1 = [m for m in a["ffn_fc1_w"]]
    fc1_b = [m for m in a["ffn_fc1_b"]]
    mult = [m for m in a["ffn_geglu_mult"]]
    fc2 = [m for m in a["ffn_fc2_w"]]
    for lo in range(0, FS, F):
        fc1.append(_np.concatenate([half(s1, lo), half(s1, FS + lo)]))
        fc1_b.append(_np.concatenate([half(s1b, lo), half(s1b, FS + lo)]))
        mult.append(half(a["ffn_s_geglu_mult"], lo))
        fc2.append(half(a["ffn_s_fc2_w"], lo, 1))

    def columns(vectors):
        v = _np.stack(vectors)
        return _np.ascontiguousarray(v.reshape(-1, P).T)

    def pack(w1, w2, b, m):
        return _np.concatenate([parts(_np.ascontiguousarray(w1.T)).reshape(P, -1),
                                parts(_np.ascontiguousarray(w2.T)).reshape(P, -1), columns([b]), columns([m])], 1)

    T = a["attn_x"].shape[0] * a["attn_x"].shape[1] // P
    restart = _np.ones((P, E, T), _np.float32)
    restart[:, :, 0] = 0
    data = {
        "x": a["attn_x"], "w_in": parts(a["attn_W_in"]),
        "conv_w": parts(_np.ascontiguousarray(a["attn_conv_w"][:, 0, :].T)), "conv_b": columns([a["attn_conv_b"]]),
        "w_x": parts(a["attn_W_x"]), "w_dt": a["attn_W_dt"], "b_dt": columns([a["attn_b_dt"]]),
        "a_log": parts(a["attn_A_log"]).reshape(P, -1), "d_skip": columns([a["attn_D"]]), "w_out": parts(a["attn_W_out"]),
        "gate_w": parts(_np.ascontiguousarray(a["ffn_gate_w"].T)),
        "packs": _np.stack([pack(*unit) for unit in zip(fc1, fc2, fc1_b, mult)]),
        "fc2_b": _np.concatenate([a["ffn_fc2_b"], a["ffn_s_fc2_b"][None]]),
        "ident": _np.eye(P, dtype=_np.float32),
        "tri": _np.triu(_np.ones((P, P), _np.float32), 1),
        "prio": _np.tile(_np.arange(E, 0, -1, dtype=_np.float32), (P, T)),
        "restart": restart.reshape(P, -1), "tiles": _np.tile(_np.arange(64, dtype=_np.float32), (P, 1)),
    }
    nc = _bacc.Bacc("TRN2", target_bir_lowering=False, num_devices=1)
    arrays, args = {}, []
    for name, v in data.items():
        v = _np.ascontiguousarray(v)
        arrays[f"in_{name}"] = v
        args.append(nc.dram_tensor(f"in_{name}", v.shape, _mybir.dt.from_np(v.dtype), kind="ExternalInput").ap())
    args.append(nc.dram_tensor("out", a["attn_x"].shape, _mybir.dt.float32, kind="ExternalOutput").ap())
    mamba_moe_block(nc, *args)
    r = _run(nc, [arrays], core_ids=[0])
    return r.results[0]["out"]
```

```python
import concourse.bass as bass
from concourse import mybir
from contextlib import ExitStack


def mamba_moe_block(nc, x, w_in, conv_w, conv_b, w_x, w_dt, b_dt, a_log, d_skip, w_out, gate_w,
                    packs, fc2_b, ident_in, tri_in, prio_in, restart_in, tiles_in, rows_in, out):
    fp32 = mybir.dt.float32
    u32 = mybir.dt.uint32
    ALU = mybir.AluOpType
    ACT = mybir.ActivationFunctionType
    AX = mybir.AxisListType

    P = 128
    B, L, DM = x.shape
    KM = DM // P
    ND = w_out.shape[1]
    DIN = ND * P
    R = w_dt.shape[0]
    N = a_log.shape[1] // ND
    XD = w_x.shape[2]
    TAPS = conv_w.shape[2]
    HALO = TAPS - 1
    TC = 512
    NT = TC // P
    CPB = L // TC
    NC = B * CPB
    TT = NC * NT
    E = gate_w.shape[2]
    TOPK = 3
    NF = 2
    F = NF * P
    W1, B1, W2, MU = 0, KM * 2 * F, KM * 2 * F + 2 * NF, KM * 2 * F + 2 * NF + NF * DM
    PACK = MU + NF
    ST = 256
    NST = ST // P
    NS = 2
    NG = N // NS
    DAR = 4
    SLOT_TILES = NC * NG
    MAXT = B * L // ST
    assert packs.shape[2] == PACK and packs.shape[0] == E + 2 and NG % 2 == 0 and NC % 2 == 0
    assert SLOT_TILES >= (TOPK * B * L + E * (ST - 1)) // ST

    xf = x.rearrange("b (t p) d -> p (b t) d", p=P)
    xc = x.rearrange("b (c t p) d -> (b c) p t d", p=P, t=NT)
    outc = out.rearrange("b (c t p) d -> (b c) p t d", p=P, t=NT)

    def dram(name, shape):
        return nc.dram_tensor(name, shape, fp32, kind="Internal").ap()

    bc_dram = dram("bc_rows", [2, 2, N, TC])
    xnT_dram = dram("xn_transposed", [NC, P, KM * TC])
    part = dram("partial_sums", [NC + 1, P, NT * DM])
    ROW = DM + 1
    TRASH = 2 * ST
    x_slots = dram("slot_inputs", [(SLOT_TILES + 1) * ST, ROW])
    y_rows = dram("expert_outputs", [TRASH + TOPK * B * L, DM])
    xsl = x_slots.rearrange("(g t p) d -> g p t d", p=P, t=NST)
    yr = y_rows[TRASH:TRASH + TOPK * B * L, :].rearrange("(k c t p) d -> k c p t d", k=TOPK, t=NT, p=P)

    ctx = ExitStack()
    with ctx:
        def sb(name, shape, dt=fp32):
            return ctx.enter_context(nc.sbuf_tensor(name, shape, dt))

        def pb(name):
            return ctx.enter_context(nc.psum_tensor(name, [P, 512], fp32))

        def sem(name):
            return ctx.enter_context(nc.semaphore(name))

        ident = sb("ident", [P, P])
        tri = sb("tri", [P, P])
        ones = sb("ones", [P, P])
        prio = sb("prio", [P, TT * E])
        restart = sb("restart", [P, E * TT])
        tiles = sb("tiles", [P, SLOT_TILES])
        rows_of = sb("rows_of", [P, NC * TOPK * NT + 2 * NST])
        win = sb("win", [P, KM, 2 * DIN])
        wx = sb("wx", [P, ND, XD])
        wdt = sb("wdt", [R, DIN])
        wout = sb("wout", [P, ND, DM])
        gw = sb("gw", [P, KM, E])
        cw = sb("cw", [P, ND, TAPS])
        cb = sb("cb", [P, ND])
        bdt = sb("bdt", [P, ND])
        al = sb("al", [P, ND * N])
        am = sb("am", [P, ND * N])
        dsk = sb("dsk", [P, ND])
        dskip = sb("dskip", [P, ND, P])
        b2 = sb("b2", [E + 1, DM])
        zero = sb("zero", [P, ROW])
        region = sb("region", [P, TT * DM])
        xall = region
        cv, u, delta, du = (region[:, i * ND * TC:(i + 1) * ND * TC].rearrange("p (d t) -> p d t", d=ND)
                            for i in range(4))
        gy = [region[:, i * TOPK * NT * DM:(i + 1) * TOPK * NT * DM].rearrange("p (k d) -> p k d", d=DM)
              for i in range(2)]
        scanbuf = sb("scanbuf", [P, (7 + DAR) * NS * TC])
        tables = [scanbuf[:, i * TT * E:(i + 1) * TT * E] for i in range(14)]

        def group(i):
            return scanbuf[:, i * NS * TC:(i + 1) * NS * TC].rearrange("p (n t) -> p n t", n=NS)

        dBu, h, hC = [group(0), group(1)], [group(2), group(3)], [group(4), group(5)]
        dA = [group(6 + i) for i in range(DAR)]
        hC.append(group(6 + DAR))
        lgT = [scanbuf[0:E, (14 + i) * TC:(15 + i) * TC] for i in range(2)]
        gated = scanbuf[:, 4 * ND * TC:5 * ND * TC].rearrange("p (d t) -> p d t", d=ND)
        spe, spw, spt, spl = (scanbuf[:, i * ND * TC:(i + 1) * ND * TC].rearrange("p (d t) -> p d t", d=ND)
                              for i in range(4))
        spreadbuf = sb("spreadbuf", [P, 4 * NT * ROW])
        stage = [spreadbuf[:, i * NT * ROW:(i + 1) * NT * ROW].rearrange("p (t d) -> p t d", d=ROW) for i in range(4)]
        Bb = [spreadbuf[:, i * NS * TC:(i + 1) * NS * TC].rearrange("p (n t) -> p n t", n=NS) for i in (0, 1)]
        Cb = [spreadbuf[:, i * NS * TC:(i + 1) * NS * TC].rearrange("p (n t) -> p n t", n=NS) for i in (2, 3)]
        st = sb("st", [P, TT * 6])
        mean = sb("mean", [P, TT])
        var = sb("var", [P, TT])
        dev = sb("dev", [P, TT])
        rstd = sb("rstd", [P, TT])
        ra = sb("ra", [P, TT])
        rb = sb("rb", [P, TT])
        top = sb("top", [P, TOPK, TT])
        comb = sb("comb", [P, TT * (E + 1)])
        cnt = sb("cnt", [P, E])
        one_e = sb("one_e", [P, E])
        incl = sb("incl", [P, E])
        base = sb("base", [P, E])
        big = sb("big", [P, SLOT_TILES * E])
        tef = sb("tef", [P, SLOT_TILES])
        te = sb("te", [P, SLOT_TILES], u32)
        slot = sb("slot", [P, NC * TOPK * NT], u32)
        wk = sb("wk", [P, NC * TOPK * NT])
        ix = [sb(f"ix{i}", [P, TOPK * NT], u32) for i in range(4)]
        xa = sb("xa", [P, 2, NT, DM])
        xnT = [sb(f"xnT{i}", [P, KM, TC]) for i in range(2)]
        xr = sb("xr", [P, ND, HALO + TC])
        sres = sb("sres", [P, ND, TC])
        xdb = sb("xdb", [XD, TC])
        combc = sb("combc", [P, NT, E + 1])
        combT = sb("combT", [E + 1, TC])
        state = sb("state", [P, ND * N])
        wp = [sb(f"wp{i}", [P, PACK]) for i in range(2)]
        w1 = [w[:, W1:B1].rearrange("p (k f) -> p k f", k=KM) for w in wp]
        w2 = [w[:, W2:MU].rearrange("p (k f) -> p k f", k=NF) for w in wp]
        act = [sb(f"act{i}", [P, NF, TC]) for i in range(2)]
        xs = [sb(f"xs{i}", [P, NST, ROW]) for i in range(2)]
        iy = [sb(f"iy{i}", [P, NST], u32) for i in range(2)]
        col = [sb(f"col{i}", [P, NST]) for i in range(2)]
        trash = [rows_of[:, NC * TOPK * NT + i * NST:NC * TOPK * NT + (i + 1) * NST] for i in range(2)]
        xsT = [sb(f"xsT{i}", [P, KM, ST]) for i in range(2)]
        ys = [sb(f"ys{i}", [P, NST, DM]) for i in range(2)]

        y = [pb(f"y{i}") for i in range(4)]
        fh = [pb(f"fh{i}") for i in range(3)]
        po = pb("po")

        s_mark = sem("waits_taken")
        s_const0 = sem("routing_constants_loaded")
        s_const = sem("constants_loaded")
        s_am = sem("decay_exponentiated")
        s_init = sem("constants_set")
        s_made = sem("constants_made")
        s_xq = [sem(f"x_quarter_{i}") for i in range(4)]
        s_v = sem("vector_steps")
        s_bn = sem("row_statistics")
        s_var = sem("variance_ready")
        s_sd = sem("deviation_ready")
        s_xn = sem("xn_ready")
        s_stage = [sem(f"rows_staged_{i}") for i in range(4)]
        s_T = sem("xn_transposed_psum")
        s_xnT = sem("xnT_copied")
        s_xts = [sem(f"xnT_stored_{i}") for i in range(2)]
        s_lsub = sem("logits_shifted")
        s_lexp = sem("logits_exponentiated")
        s_mask = sem("chosen_ready")
        s_rank = sem("ranks_ready")
        s_rkc = sem("ranks_copied")
        s_lgc = sem("logits_copied")
        s_slot = sem("slots_ready")
        s_zf = sem("slots_zeroed")
        s_st2 = [sem(f"rows_staged_for_slots_{i}") for i in range(4)]
        s_sc = [sem(f"rows_scattered_{i}") for i in range(4)]
        s_xt = [sem(f"xnT_loaded_{i}") for i in range(2)]
        s_xa = [sem(f"sums_loaded_{i}") for i in range(2)]
        s_xst = sem("sums_stored")
        s_ws = sem("shared_weights_loaded")
        s_ws2 = sem("shared_fc2_scaled")
        s_f1 = sem("shared_fc1_ready")
        s_g = sem("shared_gelu_ready")
        s_a = sem("shared_product_ready")
        s_o = sem("shared_out_ready")
        s_oc = sem("shared_out_added")
        s_zero = sem("batch_zeroed")
        s_lgT = sem("logits_made")
        s_lgTc = sem("logits_copied_to_turn")
        s_lgf = sem("logits_turned")
        s_cc = sem("chunk_weights_copied")
        s_ct = sem("weights_transposed")
        s_ctc = sem("weightsT_copied")
        s_ip = sem("inproj_ready")
        s_ipc = sem("inproj_copied")
        s_cv = sem("conv_ready")
        s_halo = sem("halo_kept")
        s_u = sem("u_ready")
        s_xd = sem("xdbl_ready")
        s_xdc = sem("xdbl_copied")
        s_bcd = sem("bc_rows_stored")
        s_bcl = [sem(f"bc_spread_{i}") for i in range(2)]
        s_dt = sem("dt_ready")
        s_spa = sem("softplus_abs")
        s_spz = sem("softplus_argument")
        s_spw = sem("softplus_sum")
        s_spt = sem("softplus_rounding")
        s_spr = sem("softplus_rounded_maximum")
        s_dup = sem("du_ready_gpsimd")
        s_spe = sem("softplus_exp")
        s_spl = sem("softplus_log")
        s_dl = sem("delta_ready")
        s_du = sem("du_ready")
        s_dA = sem("dA_ready")
        s_dBu = sem("dBu_ready")
        s_h = sem("h_ready")
        s_st = sem("state_kept")
        s_hC = sem("hC_ready")
        s_hCv = sem("last_hC_ready")
        s_ns = sem("y_accumulated")
        s_yg = sem("y_gated")
        s_co = sem("chunk_out_ready")
        s_coc = sem("chunk_out_added")
        s_mw = [sem(f"expert_fc1_weights_{i}") for i in range(2)]
        s_mv = [sem(f"expert_fc2_weights_{i}") for i in range(2)]
        s_mx = [sem(f"slot_rows_{i}") for i in range(2)]
        s_mw2 = sem("expert_fc2_scaled")
        s_mT = sem("slot_rows_transposed")
        s_mTc = sem("slot_rowsT_copied")
        s_mf = sem("expert_fc1_ready")
        s_mg = sem("expert_gelu_ready")
        s_ma = sem("expert_product_ready")
        s_m2 = sem("expert_fc2_ready")
        s_my = sem("slot_out_copied")
        s_mys = [sem(f"slot_out_scattered_{i}") for i in range(2)]
        s_row = sem("row_numbers_staged")
        s_iy0 = sem("first_output_rows_set")
        s_iy = sem("output_rows_made")
        s_col = sem("output_rows_taken")
        s_used = sem("output_rows_used")
        s_gy = [sem(f"rows_gathered_{i}") for i in range(2)]
        s_ga = sem("gathered_added")
        s_gv = sem("gathered_steps")

        ROWS = (SLOT_TILES + 1) * ST // P
        RZ = 5
        GM = ND - 1
        CR = 2 * ND
        HS = 1
        H2, H4 = 2, 4
        NCONST = 15 * 16
        INIT = 6
        VFRONT = 2
        VCONV = ND * (TAPS - 1)

        fc1_banks = (*fh, po)

        def dtbank(d):
            return y[(d + 2) % 4]

        def ybank(j):
            return (fh[1], fh[2], y[0], y[1], fh[1], fh[2], y[2], y[3])[j]

        def by_tile(t):
            return t[:, :].rearrange("p (t e) -> p t e", e=E)

        def over_e(r):
            return r.unsqueeze(2).to_broadcast([P, TT, E])

        def plain(eng):
            eng.sem_inc(s_mark, 1)

        def pairs(eng):
            plain(eng)
            with eng.Fori(0, NC // 2) as i:
                for q in range(2):
                    yield i * 2 + q, q, i

        def later_pairs(eng):
            plain(eng)
            with eng.Fori(0, NC // 2 - 1) as i:
                for q in range(2):
                    yield i * 2 + (2 + q), q, i + 1

        def fours(eng):
            plain(eng)
            with eng.Fori(0, NC // 4) as i:
                for j in range(4):
                    yield i * 4 + j, j, i

        def chunks(eng):
            plain(eng)
            with eng.Fori(0, B) as b:
                for cc in range(CPB):
                    yield b * CPB + cc, cc, b

        def groups(eng, c):
            plain(eng)
            with eng.Fori(0, NG // 2) as i:
                for q in range(2):
                    yield i * 2 + q, c * NG + i * 2 + q, q, c * (NG // 2) + i

        block = ctx.enter_context(nc.Block())

        @block.sync
        def _(sp):
            for t, src in ((ident, ident_in), (gw, gate_w)):
                sp.dma_start(t[(slice(None),) * len(t.shape)], src[(slice(None),) * len(t.shape)])\
                    .then_inc(s_const0, 16)
            for i in range(4):
                sp.dma_start(xall[:, i * 8 * DM:(i + 1) * 8 * DM].rearrange("p (t d) -> p t d", d=DM),
                             xf[:, i * 8:(i + 1) * 8, :]).then_inc(s_xq[i], 16)
            for t, src in ((tri, tri_in), (prio, prio_in), (restart, restart_in), (tiles, tiles_in), (rows_of, rows_in),
                           (win, w_in), (wx, w_x), (wdt, w_dt), (wout, w_out), (cw, conv_w), (cb, conv_b),
                           (bdt, b_dt), (al, a_log), (dsk, d_skip), (b2, fc2_b)):
                dims = (slice(None),) * len(t.shape)
                sp.dma_start(t[dims], src[dims]).then_inc(s_const, 16)
            for i in range(2):
                sp.dma_start(wp[i][:, :], packs[E + i]).then_inc(s_ws, 16)
            for c, j, turn in fours(sp):
                sp.wait_ge(s_xn, (c + 1) * NT)
                plain(sp)
                sp.wait_ge(s_T, c - 3 + CR)
                plain(sp)
                sp.dma_start(stage[j][:, :, 0:DM], xall[:, bass.ds(c * NT * DM, NT * DM)]
                             .rearrange("p (t d) -> p t d", d=DM)).then_inc(s_stage[j], 16)

            def load_sums(src, c, parity):
                sp.dma_start(xa[:, parity, :, :], src[bass.ds(c, 1)]
                             .rearrange("a p t d -> (a p) t d")).then_inc(s_xa[parity], 16)

            def store_sums(dst, c, parity, stored):
                sp.dma_start(dst[bass.ds(c, 1)].rearrange("a p t d -> (a p) t d"), xa[:, parity, :, :])\
                    .then_inc(s_xst, 16)
                sp.wait_ge(s_xst, stored * 16)
                plain(sp)

            def load_xnT(c, parity):
                sp.dma_start(xnT[parity][:, :, :], xnT_dram[bass.ds(c, 1)]
                             .rearrange("a p (k t) -> (a p) k t", k=KM)).then_inc(s_xt[parity], 16)

            partc = part.rearrange("c p (t d) -> c p t d", d=DM)
            for q in range(2):
                sp.wait_ge(s_xts[q], NC * 8 + HS)
            sp.wait_ge(s_lgf, NC + CR)
            for q in range(2):
                load_sums(xc, q, q)
                load_xnT(q, q)
            plain(sp)
            with sp.Fori(0, NC // 2 - 1) as turn:
                for q in range(2):
                    c = turn * 2 + q
                    sp.wait_ge(s_oc, (c + 1) * 4 + H4)
                    store_sums(partc, c, q, c + 1)
                    load_sums(xc, c + 2, q)
                    load_xnT(c + 2, q)
            for q in range(2):
                if q == 1:
                    for j in range(4):
                        sp.wait_ge(s_sc[j], NC * TOPK * NT * 4)
                    sp.dma_start(xs[0][:, :, :], xsl[0]).then_inc(s_mx[0], 16)
                sp.wait_ge(s_oc, (NC - 2 + q + 1) * 4 + H4)
                store_sums(partc, NC - 2 + q, q, NC - 2 + q + 1)
                if q == 0:
                    load_sums(partc, 0, 0)
                    load_xnT(0, 0)
            sp.wait_ge(s_slot, TOPK + 1)
            for c, cc, b in chunks(sp):
                sp.wait_ge(s_xdc, c + 1)
                sp.dma_start(bc_dram[cc % 2].rearrange("s n t -> (s n) t"), xdb[R:XD, :]).then_inc(s_bcd, 16)
                sp.wait_ge(s_bcd, (c + 1) * 16 + HS)
                for n, g, q, pair in groups(sp, c):
                    sp.wait_ge(s_h, (g - 1) * ND + CR)
                    sp.wait_ge(s_hC, (g - 1) * GM + CR)
                    plain(sp)
                    sp.wait_ge(s_hCv, g - 1 + H2)
                    plain(sp)
                    for k, t in enumerate((Bb, Cb)):
                        sp.dma_start(t[q], bc_dram[cc % 2, k, bass.ds(n * NS, NS), :].partition_broadcast(P))\
                            .then_inc(s_bcl[q], 16)
                    sp.wait_ge(s_ma, g - 1 + H2)
                    plain(sp)
                    e = sp.value_load(te[0:1, bass.ds(g, 1)], min_val=0, max_val=E - 1)
                    weights = packs[bass.ds(e, 1)].rearrange("a p w -> (a p) w")
                    sp.dma_start(wp[q][:, 0:W2], weights[:, 0:W2]).then_inc(s_mw[q], 16)
                    sp.wait_ge(s_mT, g + HS)
                    plain(sp)
                    sp.wait_ge(s_col, g + HS)
                    plain(sp)
                    sp.dma_start(xs[1 - q][:, :, :], xsl[bass.ds(g + 1, 1)].rearrange("a p t d -> (a p) t d"))\
                        .then_inc(s_mx[1 - q], 16)
                    sp.wait_ge(s_m2, g + CR)
                    sp.dma_start(wp[q][:, W2:PACK], weights[:, W2:PACK]).then_inc(s_mv[q], 16)
                following = c + 1 if cc < CPB - 1 else b * (-CPB) + CPB
                load_xnT(following, 1 - cc % 2)
                sp.wait_ge(s_coc, (c + 1) * 4 + HS)
                former = c - 1 if cc > 0 else b * (-(CPB + 1)) + NC
                store_sums(partc, former, 1 - cc % 2, c + 1 + NC)
                load_sums(partc, following, 1 - cc % 2)
            sp.wait_ge(s_coc, NC * 4 + 2 + HS)
            store_sums(partc, NC - 1, 1, 2 * NC + 1)
            load_sums(partc, 1, 1)
            plain(sp)
            with sp.Fori(0, NC // 2 - 1) as turn:
                for q in range(2):
                    c = turn * 2 + q
                    sp.wait_ge(s_ga, c + 1 + CR)
                    plain(sp)
                    store_sums(outc, c, q, c + 2 + 2 * NC)
                    load_sums(partc, c + 2, q)
            for q in range(2):
                sp.wait_ge(s_ga, NC - 2 + q + 1 + CR)
                store_sums(outc, NC - 2 + q, q, 3 * NC + q)
            sp.wait_ge(s_xt[0], (NC + 1) * 16)

        @block.tensor
        def _(pe):
            pe.wait_ge(s_const0, 32)
            def logits(c, j):
                pe.wait_ge(s_xnT, (c + 1) * KM + CR)
                pe.wait_ge(s_lgTc, c - 1 + H2)
                for m in range(KM):
                    mm = pe.matmul(fh[j % 2][0:E, :], gw[:, m, :], xnT[j % 2][:, m, :], start=(m == 0),
                                   stop=(m == KM - 1))
                mm.then_inc(s_lgT, 1)

            def turn_logits(c, j):
                pe.wait_ge(s_lgTc, c + 1 + H2)
                for t in range(NT):
                    mm = pe.matmul(po[:, bass.ds(c * (NT * E) + t * E, E)], lgT[j % 2][:, t * P:(t + 1) * P],
                                   ident[0:E, 0:E], start=True, stop=True)
                mm.then_inc(s_lgf, 1)

            for c, j, turn in fours(pe):
                pe.wait_ge(s_stage[j], (turn + 1) * 16)
                pe.wait_ge(s_xnT, (c - 1) * KM + CR)
                for t in range(NT):
                    for m in range(KM):
                        mm = pe.transpose(y[2 * (j % 2) + m][:, t * P:(t + 1) * P],
                                          stage[j][:, t, m * P:(m + 1) * P], ident[:, :])
                mm.then_inc(s_T, 1)
                if j > 0:
                    logits(c - 1, j - 1)
                if j > 1:
                    turn_logits(c - 2, j - 2)
                if j == 3:
                    logits(c, j)
                    turn_logits(c - 1, j - 1)
                    turn_logits(c, j)
            def rank():
                pe.wait_ge(s_init, INIT)
                pe.wait_ge(s_mask, 1)
                pe.wait_ge(s_oc, 4 + H4)
                pe.matmul(y[2][:, 0:TT * E], tri[:, :], tables[3], start=True, stop=True).then_inc(s_rank, 1)
                pe.matmul(y[3][:, 0:TT * E], ones[:, :], tables[3], start=True, stop=True).then_inc(s_rank, 1)

            def shared(c, q, turn, with_ranks=False):
                for i in range(2):
                    if with_ranks and i == 1:
                        rank()
                    w = c * 2 + i
                    if i == 0:
                        pe.wait_ge(s_xt[q], (turn + 1) * 16)
                    for k, ft in enumerate((NF, NF + 1, 0, 1)):
                        pe.wait_ge(s_g if k < NF else s_a, (w - 1) * NF + k % NF + 1 + H2)
                        for m in range(KM):
                            mm = pe.matmul(fc1_banks[k][:, :], w1[i][:, m, ft * P:(ft + 1) * P], xnT[q][:, m, :],
                                           start=(m == 0), stop=(m == KM - 1))
                        mm.then_inc(s_f1, 1)
                for i in range(2):
                    if with_ranks and i == 1:
                        pe.wait_ge(s_rkc, 1)
                    pe.wait_ge(s_a, (c * 2 + i + 1) * NF + H2)
                    for half in range(2):
                        pe.wait_ge(s_oc, c * 4 + i * 2 + half - 3 + H4)
                        for t in range(2):
                            tok = (half * 2 + t) * P
                            for f in range(NF):
                                mm = pe.matmul(y[i * 2 + half][:, t * DM:(t + 1) * DM], act[i][:, f, tok:tok + P], w2[i][:, f, :],
                                               start=(f == 0), stop=(f == NF - 1))
                        mm.then_inc(s_o, 1)

            pe.wait_ge(s_const, NCONST)
            pe.wait_ge(s_lgc, 1)
            pe.wait_ge(s_ws2, 2)
            shared(0, 0, 0)
            shared(1, 1, 0, with_ranks=True)
            for c, q, turn in later_pairs(pe):
                shared(c, q, turn)

            def state_sum(d, g):
                if d < GM:
                    pe.wait_ge(s_hC, g * GM + d + 1 + CR)
                else:
                    pe.wait_ge(s_hCv, g + 1 + H2)
                for i in range(NS):
                    mm = pe.matmul(y[d][:, :], ident[:, :], hC[d % 2 if d < GM else 2][:, i, :], start=False, stop=False,
                                   skip_group_check=True)
                mm.then_inc(s_ns, 1)

            pe.wait_ge(s_made, 1 + ND)
            def turn_rows(i, arrived):
                pe.wait_ge(s_mx[i], arrived)
                for t in range(NST):
                    for m in range(KM):
                        mm = pe.transpose(fh[0][:, m * ST + t * P:m * ST + (t + 1) * P],
                                          xs[i][:, t, m * P:(m + 1) * P], ident[:, :])
                mm.then_inc(s_mT, 1)

            def expert_in(i, bank, first):
                for f in range(NF):
                    ft = first + f
                    for m in range(KM):
                        mm = pe.matmul(fh[bank][:, f * ST:(f + 1) * ST], w1[i][:, m, ft * P:(ft + 1) * P],
                                       xsT[i][:, m, :], start=(m == 0), stop=(m == KM - 1))
                mm.then_inc(s_mf, 1)

            def expert_out(i):
                for t in range(NST):
                    for f in range(NF):
                        mm = pe.matmul(po[:, t * DM:(t + 1) * DM], act[i][:, f, t * P:(t + 1) * P], w2[i][:, f, :],
                                       start=(f == 0), stop=(f == NF - 1))
                mm.then_inc(s_m2, 1)

            def project(c):
                pe.wait_ge(s_yg, (c + 1) * ND + H4)
                for half in range(2):
                    for t in range(2):
                        tok = (half * 2 + t) * P
                        for d in range(ND):
                            mm = pe.matmul(fh[1 + half][:, t * DM:(t + 1) * DM], gated[:, d, tok:tok + P], wout[:, d, :],
                                           start=(d == 0), stop=(d == ND - 1))
                    mm.then_inc(s_co, 1)

            pe.wait_ge(s_oc, NC * 4 + H4)
            turn_rows(0, 16)
            for c, cc, b in chunks(pe):
                pe.wait_ge(s_xt[cc % 2], (b * (CPB // 2) + (cc // 2 + 1 + NC // 2)) * 16)
                pe.wait_ge(s_ma, c * NG + H2)
                def in_project(j, former):
                    if former is not None:
                        pe.wait_ge(s_ipc, c * 2 * ND + former + 1)
                    for m in range(KM):
                        mm = pe.matmul(ybank(j)[:, :], win[:, m, j * P:(j + 1) * P], xnT[cc % 2][:, m, :],
                                       start=(m == 0), stop=(m == KM - 1))
                    mm.then_inc(s_ip, 1)

                in_project(0, None)
                in_project(1, None)
                pe.wait_ge(s_yg, c * ND - 2 + H4)
                in_project(2, None)
                in_project(3, None)
                in_project(4, 0)
                in_project(5, 1)
                pe.wait_ge(s_yg, c * ND + H4)
                in_project(6, None)
                in_project(7, None)
                pe.wait_ge(s_ipc, (c + 1) * 2 * ND)
                for d in range(ND):
                    pe.wait_ge(s_u, c * ND + d + 1)
                    mm = pe.matmul(y[0][0:XD, :], wx[:, d, :], u[:, d, :], start=(d == 0), stop=(d == ND - 1))
                mm.then_inc(s_xd, 1)
                pe.wait_ge(s_cc, c + 1)
                for t in range(NT):
                    mm = pe.transpose(y[1][0:E + 1, t * P:(t + 1) * P], combc[:, t, :], ident[:, :])
                mm.then_inc(s_ct, 1)
                pe.wait_ge(s_xdc, c + 1)
                for d in range(ND):
                    if d == ND - 1:
                        pe.wait_ge(s_ctc, c + 1 + HS)
                    pe.matmul(dtbank(d)[:, :], wdt[:, d * P:(d + 1) * P], xdb[0:R, :],
                              start=True, stop=True).then_inc(s_dt, 1)
                for half in range(2):
                    for t in range(2):
                        tok = (half * 2 + t) * P
                        mm = pe.matmul(fh[1 + half][:, t * DM:(t + 1) * DM], combT[:, tok:tok + P], b2[:, :],
                                       start=True, stop=True)
                    mm.then_inc(s_co, 1)
                pe.wait_ge(s_coc, c * 4 + 2 + HS)
                project(c - 1)
                pe.wait_ge(s_spz, (c + 1) * ND)
                for d in range(ND):
                    pe.matmul(y[d][:, :], dskip[:, d, :], u[:, d, :], start=True, stop=False,
                              skip_group_check=True)
                pe.wait_ge(s_coc, (c + 1) * 4 + HS)
                for n, g, q, pair in groups(pe, c):
                    pe.wait_ge(s_mTc, g + 1)
                    pe.wait_ge(s_mw[q], (pair + 1) * 16)
                    pe.wait_ge(s_ma, g + H2)
                    expert_in(q, 1, NF)
                    turn_rows(1 - q, (pair + 1 + q) * 16)
                    state_sum(0, g)
                    expert_in(q, 2, 0)
                    state_sum(1, g)
                    pe.wait_ge(s_mw2, g + HS)
                    pe.wait_ge(s_my, g + 1 + HS)
                    expert_out(1 - q)
                    state_sum(2, g)
                    state_sum(3, g)
            pe.wait_ge(s_my, SLOT_TILES + 1 + HS)
            pe.wait_ge(s_mw2, SLOT_TILES + HS)
            pe.wait_ge(s_ma, SLOT_TILES + H2)
            expert_out(1)
            project(NC - 1)

        @block.scalar
        def _(sa):
            sa.wait_ge(s_var, 1)
            sa.activation(dev[:, :], var[:, :], ACT.Sqrt).then_inc(s_sd, 1)
            sa.wait_ge(s_init, INIT)
            slots_by_p = x_slots.rearrange("(p r) d -> p r d", p=P)

            def zero_fill(first, rows):
                sa.dma_start(slots_by_p[:, bass.ds(first, rows), :], zero[:, :].unsqueeze(1).to_broadcast([P, rows, ROW]))\
                    .then_inc(s_zf, 16)

            def copy_logits(c, j):
                sa.wait_ge(s_lgT, c + 1 + H2)
                sa.wait_ge(s_lgf, c - 1 + CR)
                sa.activation(lgT[j % 2], fh[j % 2][0:E, :], ACT.Copy).then_inc(s_lgTc, 1)

            for c, j, turn in fours(sa):
                q = j % 2
                sa.wait_ge(s_T, c + 1 + CR)
                sa.wait_ge(s_lgT, c - 1 + H2)
                sa.wait_ge(s_xts[q], (turn * 2 + j // 2) * 16 + HS)
                for m in range(KM):
                    sa.activation(xnT[q][:, m, :], y[2 * q + m][:, :], ACT.Copy).then_inc(s_xnT, 1)
                sa.wait_ge(s_xnT, (c + 1) * KM + CR)
                sa.dma_start(xnT_dram[bass.ds(c, 1)].rearrange("a p (k t) -> (a p) k t", k=KM), xnT[q][:, :, :])\
                    .then_inc(s_xts[q], 16)
                zero_fill(c * RZ, RZ)
                if j > 0:
                    copy_logits(c - 1, j - 1)
                if j == 3:
                    copy_logits(c, j)
            sa.wait_ge(s_lsub, 1)
            sa.activation(tables[1], tables[1], ACT.Exp).then_inc(s_lexp, 1)
            sa.wait_ge(s_const, NCONST)
            sa.activation(am[:, :], al[:, :], ACT.Exp).then_inc(s_am, 1)
            for q in range(2):
                sa.wait_ge(s_xt[q], 16)
            zero_fill(NC * RZ, ROWS - NC * RZ)

            for c, q, turn in pairs(sa):
                for i in range(2):
                    w = c * 2 + i
                    sa.wait_ge(s_oc, c * 4 + i * 2 - 2 + H4)
                    for f in range(NF):
                        sa.wait_ge(s_f1, w * 2 * NF + f + 1)
                        sa.activation(act[i][:, f, :], fh[f][:, :], ACT.Gelu,
                                      bias=wp[i][:, B1 + NF + f:B1 + NF + f + 1]).then_inc(s_g, 1)

            def copy_rowsT(i, g):
                sa.wait_ge(s_mT, g + 1 + HS)
                sa.activation(xsT[i][:, :, :], fh[0][:, :].rearrange("p (k s) -> p k s", k=KM), ACT.Copy)\
                    .then_inc(s_mTc, 1)

            def copy_out(g, q):
                sa.wait_ge(s_m2, g + CR)
                sa.wait_ge(s_used, g - 1 + H2)
                sa.activation(ys[q][:, :, :], po[:, :].rearrange("p (t d) -> p t d", d=DM), ACT.Copy)\
                    .then_inc(s_my, 1)

            sa.wait_ge(s_made, 1 + ND)
            sa.wait_ge(s_oc, NC * 4 + H4)
            for c, cc, b in chunks(sa):
                sa.wait_ge(s_halo, c + HS)
                def take(j):
                    sa.wait_ge(s_ip, c * 2 * ND + j + 1)
                    if j < ND:
                        i = sa.activation(xr[:, j, HALO:], ybank(j)[:, :], ACT.Copy)
                    else:
                        i = sa.activation(sres[:, j - ND, :], ybank(j)[:, :], ACT.Silu)
                    i.then_inc(s_ipc, 1)

                def conv_silu(d):
                    sa.wait_ge(s_cv, c * ND + d + 1)
                    sa.activation(u[:, d, :], cv[:, d, :], ACT.Silu).then_inc(s_u, 1)

                for j in range(ND):
                    take(j)
                take(4)
                take(5)
                conv_silu(0)
                conv_silu(1)
                take(6)
                take(7)
                conv_silu(2)
                conv_silu(3)
                sa.wait_ge(s_xd, c + 1)
                sa.wait_ge(s_bcd, c * 16 + HS)
                sa.activation(xdb[:, :], y[0][0:XD, :], ACT.Copy).then_inc(s_xdc, 1)
                sa.wait_ge(s_ct, c + 1)
                sa.activation(combT[:, :], y[1][0:E + 1, :], ACT.Copy).then_inc(s_ctc, 1)
                for d in range(ND):
                    sa.wait_ge(s_dt, c * ND + d + 1)
                    sa.activation(spe[:, d, :], dtbank(d)[:, :], ACT.Abs, bias=bdt[:, d:d + 1]).then_inc(s_spa, 1)
                for d in range(ND):
                    sa.wait_ge(s_spa, c * ND + d + 1)
                    sa.activation(spe[:, d, :], spe[:, d, :], ACT.Exp, scale=-1.0).then_inc(s_spe, 1)
                for d in range(ND):
                    sa.wait_ge(s_spw, c * ND + d + 1)
                    sa.activation(spl[:, d, :], spw[:, d, :], ACT.Ln).then_inc(s_spl, 1)
                sa.wait_ge(s_co, (c + 1) * 4 + HS)
                sa.wait_ge(s_dl, (c + 1) * ND)

                def decay(d, g, n):
                    sa.wait_ge(s_h, g * ND + d - (DAR - 1) + CR)
                    for i in range(NS):
                        e = sa.activation(dA[d % DAR][:, i, :], delta[:, d, :], ACT.Exp,
                                          scale=am[:, bass.ds(n * NS + (d * N + i), 1)])
                    e.then_inc(s_dA, 1)

                for n, g, q, pair in groups(sa, c):
                    copy_rowsT(q, g)
                    decay(0, g, n)
                    decay(1, g, n)
                    decay(2, g, n)
                    copy_out(g, q)
                    decay(3, g, n)
                    sa.wait_ge(s_mv[q], (pair + 1) * 16)
                    for f in range(NF):
                        e = sa.activation(w2[q][:, f, :], w2[q][:, f, :], ACT.Copy, scale=wp[q][:, MU + f:MU + f + 1])
                    e.then_inc(s_mw2, 1)
                    sa.wait_ge(s_mf, g * 2 + 1)
                    sa.wait_ge(s_m2, g + CR)
                    for f in range(NF):
                        e = sa.activation(act[q][:, f, 0:ST], fh[1][:, f * ST:(f + 1) * ST], ACT.Gelu,
                                          bias=wp[q][:, B1 + NF + f:B1 + NF + f + 1])
                    e.then_inc(s_mg, 1)
            for i in range(2):
                copy_out(SLOT_TILES + i, i)
            for q in range(2):
                sa.wait_ge(s_mys[q], (SLOT_TILES // 2 + 1) * NST * 16)
            sa.wait_ge(s_yg, NC * ND + H4)
            for c, q, turn in pairs(sa):
                sa.wait_ge(s_ga, c - 1 + CR)
                plain(sa)
                for k in range(TOPK):
                    sa.dma_start(gy[q][:, k * NT:(k + 1) * NT, :], yr[k, bass.ds(c, 1)]
                                 .rearrange("a p t d -> (a p) t d")).then_inc(s_gy[q], 16)

        @block.gpsimd
        def _(gp):
            gp.memset(zero[:, :], 0.0).then_inc(s_init, 1)
            gp.memset(ones[:, :], 1.0).then_inc(s_init, 1)
            gp.memset(one_e[:, :], 1.0).then_inc(s_init, 1)
            gp.memset(comb[:, :], 1.0).then_inc(s_init, 1)
            gp.memset(gated, 0.0).then_inc(s_init, 1)
            gp.memset(col[1][:, :], 0.0).then_inc(s_init, 1)
            for q in (s_T, s_xnT, s_lgf, s_ga, s_h, s_hC, s_ns, s_m2):
                gp.sem_inc(q, CR)
            for q in (s_g, s_a, s_ma, s_hCv, s_st, s_iy, s_used, s_lgT, s_lgTc):
                gp.sem_inc(q, H2)
            for q in (s_oc, s_yg):
                gp.sem_inc(q, H4)
            for q in (s_halo, s_col, s_bcd, s_coc, s_ctc, s_mT, s_mw2, s_my, s_co):
                gp.sem_inc(q, HS)
            for q in s_xts:
                gp.sem_inc(q, HS)

            gp.wait_ge(s_T, NC + CR)
            gp.wait_ge(s_zf, (NC + 1) * 16)
            plain(gp)
            with gp.Fori(0, NC // 4) as turn:
                for j in range(4):
                    c = turn * 4 + j
                    gp.dma_start(stage[j][:, :, 0:DM], xall[:, bass.ds(c * NT * DM, NT * DM)]
                                 .rearrange("p (t d) -> p t d", d=DM)).then_inc(s_st2[j], 16)
                plain(gp)
                for k in range(TOPK):
                    gp.wait_ge(s_slot, k + 1)
                    plain(gp)
                    for j in range(4):
                        c = turn * 4 + j
                        at = bass.ds(c * (TOPK * NT) + k * NT, NT)
                        if k == 0:
                            gp.wait_ge(s_st2[j], (turn + 1) * 16)
                        else:
                            gp.wait_ge(s_sc[j], turn * (TOPK * NT * 16) + k * (NT * 16))
                        plain(gp)
                        gp.tensor_copy(ix[j][:, k * NT:(k + 1) * NT], slot[:, at]).then_inc(s_row, 1)
                        gp.tensor_copy(stage[j][:, :, DM], rows_of[:, at]).then_inc(s_row, 1)
                        gp.wait_ge(s_row, turn * (TOPK * 8) + k * 8 + 2 * j + 2)
                        plain(gp)
                        for t in range(NT):
                            gp.indirect_dma_start(x_slots[:, :],
                                                  bass.IndirectOffsetOnAxis(ix[j][:, k * NT + t:k * NT + t + 1], 0),
                                                  stage[j][:, t, :], None).then_inc(s_sc[j], 16)
                for j in range(4):
                    gp.wait_ge(s_sc[j], (turn + 1) * (TOPK * NT * 16))
                plain(gp)
            gp.tensor_copy(iy[0][:, :], trash[0]).then_inc(s_iy0, 1)
            gp.wait_ge(s_iy0, 1)

            def scatter(g, q):
                gp.wait_ge(s_my, g + 1 + HS)
                plain(gp)
                gp.wait_ge(s_iy, g + H2)
                plain(gp)
                for t in range(NST):
                    gp.indirect_dma_start(y_rows[:, :], bass.IndirectOffsetOnAxis(iy[q][:, t:t + 1], 0),
                                          ys[q][:, t, :], None).then_inc(s_mys[q], 16)

            for c, cc, b in chunks(gp):
                for d in range(2):
                    gp.wait_ge(s_spz, c * ND + d + 1)
                    gp.wait_ge(s_spt, c * ND + d + 1)
                    gp.tensor_tensor(spt[:, d, :], delta[:, d, :], spt[:, d, :], ALU.subtract).then_inc(s_spr, 1)
                for d in range(2):
                    gp.wait_ge(s_dl, c * ND + d + 1)
                    gp.tensor_tensor(du[:, d, :], delta[:, d, :], u[:, d, :], ALU.mult).then_inc(s_dup, 1)
                for n, g, q, pair in groups(gp, c):
                    gp.wait_ge(s_bcl[q], (pair + 1) * 32)
                    for d in range(GM):
                        if d == 2:
                            scatter(g, q)
                        k = g * ND + d
                        gp.wait_ge(s_h, k + 1 + CR)
                        gp.wait_ge(s_ns, k - (3 if d == 1 else 1) + CR)
                        gp.tensor_tensor(hC[d % 2], h[d % 2], Cb[q], ALU.mult).then_inc(s_hC, 1)
                    gp.wait_ge(s_mys[q], (pair + 1) * (NST * 16))
                    gp.sem_inc(s_used, 1)
            for i in range(2):
                scatter(SLOT_TILES + i, i)

        @block.vector
        def _(dv):
            class Steps:
                before, steps = 0, 0

                def done(self, ins):
                    ins.then_inc(s_v, 1)
                    self.steps += 1

                def settle(self):
                    dv.wait_ge(s_v, self.before + self.steps)

                def chain(self, ins):
                    self.done(ins)
                    self.settle()

            fr = Steps()
            for i in range(4):
                dv.wait_ge(s_xq[i], 16)
                plain(dv)
                with dv.Fori(0, TT // 16) as t:
                    for k in range(4):
                        j = t * 4 + (i * (TT // 4) + k)
                        dv.bn_stats(st[:, bass.ds(j * 6, 6)], xall[:, bass.ds(j * DM, DM)]).then_inc(s_bn, 1)
            dv.wait_ge(s_bn, TT)
            s6 = st[:, :].rearrange("p (t k) -> p t k", k=6)
            m_even, v_even, m_odd, v_odd = (s6[:, :, k] for k in (1, 2, 4, 5))
            fr.chain(dv.tensor_tensor(ra[:, :], m_even, m_odd, ALU.subtract))
            fr.chain(dv.tensor_tensor(rb[:, :], ra[:, :], ra[:, :], ALU.mult))
            fr.chain(dv.tensor_scalar(rb[:, :], rb[:, :], 0.25, 1e-5, ALU.mult, ALU.add))
            fr.chain(dv.tensor_tensor(ra[:, :], v_even, v_odd, ALU.add))
            dv.scalar_tensor_tensor(out=var[:, :], in0=ra[:, :], scalar=1.0 / DM, in1=rb[:, :], op0=ALU.mult,
                                    op1=ALU.add).then_inc(s_var, 1)
            fr.chain(dv.tensor_tensor(mean[:, :], m_even, m_odd, ALU.add))
            fr.chain(dv.tensor_scalar(mean[:, :], mean[:, :], 0.5, None, ALU.mult))
            dv.wait_ge(s_sd, 1)
            fr.chain(dv.reciprocal(rstd[:, :], dev[:, :]))
            plain(dv)
            with dv.Fori(0, TT // 4) as t:
                for k in range(4):
                    j = t * 4 + k
                    row = xall[:, bass.ds(j * DM, DM)]
                    dv.tensor_scalar(row, row, mean[:, bass.ds(j, 1)], rstd[:, bass.ds(j, 1)], ALU.subtract,
                                     ALU.mult).then_inc(s_xn, 1)
            dv.wait_ge(s_const, NCONST)
            for d in range(ND):
                dv.tensor_scalar(dskip[:, d, :], ident[:, :], dsk[:, d:d + 1], None, ALU.mult).then_inc(s_made, 1)
            dv.wait_ge(s_ws, 32)

            def scale_w2(i, inc_sem):
                for f in range(NF):
                    m = dv.tensor_scalar(w2[i][:, f, :], w2[i][:, f, :], wp[i][:, MU + f:MU + f + 1], None, ALU.mult)
                m.then_inc(inc_sem, 1)

            for i in range(2):
                scale_w2(i, s_ws2)

            sc, lg, sm, mask = (by_tile(tables[i]) for i in range(4))
            oh = [by_tile(tables[4 + k]) for k in range(TOPK)]
            eq, tot, inc, exc, pos = (tables[7 + i] for i in range(5))
            pr = by_tile(prio)

            def choose(k):
                left = sm if k else sc
                fr.chain(dv.tensor_reduce(top[:, k, :], left, AX.X, ALU.max))
                fr.chain(dv.tensor_tensor(by_tile(eq), left, over_e(top[:, k, :]), ALU.is_equal))
                fr.chain(dv.tensor_tensor(by_tile(eq), by_tile(eq), pr, ALU.mult))
                fr.chain(dv.tensor_reduce(rb[:, :], by_tile(eq), AX.X, ALU.max))
                fr.chain(dv.tensor_tensor(oh[k], by_tile(eq), over_e(rb[:, :]), ALU.is_equal))
                fr.chain(dv.scalar_tensor_tensor(out=tables[2], in0=tables[4 + k], scalar=-2.0,
                                                 in1=tables[2] if k else tables[0], op0=ALU.mult, op1=ALU.add))

            def multiply(c, i):
                for f in range(NF):
                    w = c * 2 + i
                    dv.wait_ge(s_f1, w * 2 * NF + NF + f + 1)
                    dv.wait_ge(s_g, w * NF + f + 1 + H2)
                    a = act[i][:, f, :]
                    dv.scalar_tensor_tensor(out=a, in0=fc1_banks[NF + f][:, :], scalar=wp[i][:, B1 + f:B1 + f + 1],
                                            in1=a, op0=ALU.add, op1=ALU.mult).then_inc(s_a, 1)

            def add_shared(c, q, turn, i):
                dv.wait_ge(s_xa[q], (turn + 1) * 16)
                for k in (2 * i, 2 * i + 1):
                    dv.wait_ge(s_o, c * 4 + k + 1)
                    dv.wait_ge(s_oc, c * 4 + k + H4)
                    half = k % 2
                    rows = xa[:, q, 2 * half:2 * half + 2, :]
                    dv.tensor_tensor(rows, rows, y[k][:, :].rearrange("p (t d) -> p t d", d=DM), ALU.add)\
                        .then_inc(s_oc, 1)

            dv.wait_ge(s_lgf, NC + CR)
            fr.chain(dv.tensor_copy(tables[0], po[:, 0:TT * E]))
            dv.sem_inc(s_lgc, 1)
            fr.chain(dv.tensor_reduce(ra[:, :], sc, AX.X, ALU.max))
            dv.tensor_tensor(lg, sc, over_e(ra[:, :]), ALU.subtract).then_inc(s_lsub, 1)
            dv.wait_ge(s_lexp, 1)
            fr.chain(dv.tensor_reduce(ra[:, :], lg, AX.X, ALU.add))
            fr.chain(dv.reciprocal(rb[:, :], ra[:, :]))
            fr.chain(dv.tensor_tensor(sc, lg, over_e(rb[:, :]), ALU.mult))
            multiply(0, 0)
            choose(0)
            choose(1)
            multiply(0, 1)
            choose(2)
            add_shared(0, 0, 0, 0)
            dv.tensor_scalar(tables[3], tables[2], 0.0, None, ALU.is_lt).then_inc(s_mask, 1)
            fr.chain(dv.tensor_tensor(ra[:, :], top[:, 0, :], top[:, 1, :], ALU.add))
            fr.chain(dv.tensor_tensor(ra[:, :], ra[:, :], top[:, 2, :], ALU.add))
            fr.chain(dv.tensor_scalar(ra[:, :], ra[:, :], 1e-20, None, ALU.add))
            fr.chain(dv.reciprocal(rb[:, :], ra[:, :]))
            wk4 = wk[:, :].rearrange("p (c k t) -> p k c t", k=TOPK, t=NT)
            for k in range(TOPK):
                fr.done(dv.tensor_tensor(wk4[:, k], top[:, k, :].rearrange("p (c t) -> p c t", t=NT),
                                         rb[:, :].rearrange("p (c t) -> p c t", t=NT), ALU.mult))
            fr.chain(dv.tensor_tensor(by_tile(eq), sc, mask, ALU.mult))
            fr.chain(dv.tensor_tensor(comb[:, :].rearrange("p (t e) -> p t e", e=E + 1)[:, :, 0:E], by_tile(eq),
                                      over_e(rb[:, :]), ALU.mult))
            add_shared(0, 0, 0, 1)
            multiply(1, 0)
            dv.wait_ge(s_rank, 2)
            by_e = "p (t e) -> p e t"
            fr.chain(dv.tensor_copy(pos, y[2][:, 0:TT * E]))
            fr.chain(dv.tensor_copy(tot.rearrange("p (e t) -> p e t", e=E), y[3][:, 0:TT * E].rearrange(by_e, e=E)))
            dv.sem_inc(s_rkc, 1)
            fr.chain(dv.tensor_tensor_scan(inc, restart[:, :], tot, 0.0, ALU.mult, ALU.add))
            fr.chain(dv.tensor_tensor(exc, inc, tot, ALU.subtract))
            n_e = inc.rearrange("p (e t) -> p e t", e=E)[:, :, TT - 1:TT]
            fr.chain(dv.tensor_scalar(tef[:, 0:MAXT], tiles[:, 0:MAXT], float(ST), None, ALU.mult))
            cmp = big[:, 0:E * MAXT].rearrange("p (e m) -> p e m", e=E)
            fr.chain(dv.tensor_tensor(cmp, n_e.to_broadcast([P, E, MAXT]),
                                      tef[:, 0:MAXT].unsqueeze(1).to_broadcast([P, E, MAXT]), ALU.is_gt))
            fr.chain(dv.tensor_reduce(cnt[:, :], cmp, AX.X, ALU.add))
            multiply(1, 1)
            fr.chain(dv.tensor_tensor_scan(incl[:, :], one_e[:, :], cnt[:, :], 0.0, ALU.mult, ALU.add))
            fr.chain(dv.tensor_tensor(base[:, :], incl[:, :], cnt[:, :], ALU.subtract))
            fr.chain(dv.tensor_scalar(base[:, :], base[:, :], float(ST), None, ALU.mult))
            fr.chain(dv.tensor_tensor(exc.rearrange("p (e t) -> p e t", e=E), exc.rearrange("p (e t) -> p e t", e=E),
                                      base[:, :].unsqueeze(2).to_broadcast([P, E, TT]), ALU.add))
            fr.chain(dv.tensor_tensor(by_tile(pos), exc.rearrange("p (e t) -> p t e", e=E),
                                      by_tile(pos), ALU.add))
            add_shared(1, 1, 0, 0)
            slot4 = slot[:, :].rearrange("p (c k t) -> p k c t", k=TOPK, t=NT)
            for k in range(TOPK):
                fr.chain(dv.tensor_tensor(by_tile(eq), by_tile(pos), oh[k], ALU.mult))
                fr.chain(dv.tensor_reduce(ra[:, :], by_tile(eq), AX.X, ALU.add))
                dv.tensor_copy(slot4[:, k], ra[:, :].rearrange("p (c t) -> p c t", t=NT)).then_inc(s_slot, 1)
                dv.wait_ge(s_slot, k + 1)
            add_shared(1, 1, 0, 1)
            big3 = big[:, :].rearrange("p (g e) -> p g e", e=E)
            fr.chain(dv.tensor_tensor(big3, tiles[:, :].unsqueeze(2).to_broadcast([P, SLOT_TILES, E]),
                                      incl[:, :].unsqueeze(1).to_broadcast([P, SLOT_TILES, E]), ALU.is_ge))
            fr.chain(dv.tensor_reduce(tef[:, :], big3, AX.X, ALU.add))
            dv.tensor_scalar(te[:, :], tef[:, :], float(E - 1), None, ALU.min).then_inc(s_slot, 1)
            dv.wait_ge(s_am, 1)
            dv.tensor_scalar(am[:, :], am[:, :], -1.0, None, ALU.mult).then_inc(s_made, 1)

            for c, q, turn in later_pairs(dv):
                for i in range(2):
                    multiply(c, i)
                for i in range(2):
                    add_shared(c, q, turn, i)

            def drive(d, g, q):
                dv.tensor_tensor(dBu[d % 2], du[:, d:d + 1, :].to_broadcast([P, NS, TC]), Bb[q], ALU.mult)\
                    .then_inc(s_dBu, 1)

            def scan(d, g, n):
                k = g * ND + d
                dv.wait_ge(s_dBu, k + 1)
                dv.wait_ge(s_dA, k + 1)
                dv.wait_ge(s_st, k - 1 + H2)
                if d == 1:
                    dv.wait_ge(s_hCv, g + H2)
                else:
                    dv.wait_ge(s_hC, g * GM + (0, None, 1, 2)[d] + CR)
                for i in range(NS):
                    at = bass.ds(n * NS + (d * N + i), 1)
                    hs = dv.tensor_tensor_scan(h[d % 2][:, i, :], dA[d % DAR][:, i, :], dBu[d % 2][:, i, :],
                                               state[:, at], ALU.mult, ALU.add)
                hs.then_inc(s_h, 1)

            def output_rows(i, g):
                dv.wait_ge(s_used, g + H2)
                dv.tensor_tensor(iy[i][:, :], col[i][:, :], trash[i], ALU.max).then_inc(s_iy, 1)

            def take_rows(q, pair):
                dv.wait_ge(s_mx[q], (pair + 1) * 16)
                plain(dv)
                dv.tensor_copy(col[q][:, :], xs[q][:, :, DM]).then_inc(s_col, 1)

            def keep(d, g, n):
                dv.wait_ge(s_h, g * ND + d + 1 + CR)
                plain(dv)
                dv.tensor_copy(state[:, bass.ds(n * NS + d * N, NS)], h[d % 2][:, :, TC - 1]).then_inc(s_st, 1)

            def add_out(q, k, before):
                dv.wait_ge(s_co, before + 1 + HS)
                dv.wait_ge(s_coc, before + HS)
                half = k % 2
                rows = xa[:, q, 2 * half:2 * half + 2, :]
                dv.tensor_tensor(rows, rows, fh[1 + half][:, :].rearrange("p (t d) -> p t d", d=DM), ALU.add)\
                    .then_inc(s_coc, 1)

            before = fr.steps
            for j in range(4):
                dv.wait_ge(s_sc[j], NC * TOPK * NT * 4)
            for c, cc, b in chunks(dv):
                fr.before, fr.steps = before + c * (VFRONT + VCONV), 0
                dv.wait_ge(s_ctc, c + HS)
                plain(dv)
                dv.tensor_copy(combc[:, :, :], comb[:, bass.ds(c * (NT * (E + 1)), NT * (E + 1))]
                               .rearrange("p (t e) -> p t e", e=E + 1)).then_inc(s_cc, 1)
                if cc == 0:
                    dv.wait_ge(s_halo, c + HS)
                    dv.wait_ge(s_st, c * (NG * ND) + H2)
                    dv.memset(xr[:, :, 0:HALO], 0.0).then_inc(s_zero, 1)
                    dv.memset(state[:, :], 0.0).then_inc(s_zero, 1)
                    dv.wait_ge(s_zero, (b + 1) * 2)
                for pair in range(0, ND, 2):
                    for d in (pair, pair + 1):
                        dv.wait_ge(s_ipc, c * 2 * ND + d + 1)
                        fr.done(dv.tensor_scalar(cv[:, d, :], xr[:, d, 0:TC], cw[:, d, 0:1], cb[:, d:d + 1],
                                                 ALU.mult, ALU.add))
                    for k in range(1, TAPS):
                        for d in (pair, pair + 1):
                            dv.wait_ge(s_v, fr.before + fr.steps - 1 + (d - pair if k == TAPS - 1 else 0))
                            s = dv.scalar_tensor_tensor(out=cv[:, d, :], in0=xr[:, d, k:k + TC],
                                                        scalar=cw[:, d, k:k + 1], in1=cv[:, d, :], op0=ALU.mult,
                                                        op1=ALU.add)
                            if k < TAPS - 1:
                                fr.done(s)
                            else:
                                s.then_inc(s_cv, 1)
                dv.wait_ge(s_cv, (c + 1) * ND)
                dv.tensor_copy(xr[:, :, 0:HALO], xr[:, :, TC:TC + HALO]).then_inc(s_halo, 1)
                for d in range(ND):
                    dv.wait_ge(s_spa, c * ND + d + 1)
                    dv.tensor_scalar(delta[:, d, :], dtbank(d)[:, :], bdt[:, d:d + 1], 0.0, ALU.add, ALU.max)\
                        .then_inc(s_spz, 1)
                dv.wait_ge(s_xa[cc % 2], (b * (CPB // 2) + (cc // 2 + 1 + NC // 2)) * 16)
                for k in range(2):
                    add_out(cc % 2, k, c * 4 + k)
                for d in range(ND):
                    dv.wait_ge(s_spe, c * ND + d + 1)
                    dv.tensor_scalar(spw[:, d, :], spe[:, d, :], 1.0, None, ALU.add).then_inc(s_spw, 1)
                for d in range(ND):
                    dv.wait_ge(s_spw, c * ND + d + 1)
                    dv.scalar_tensor_tensor(out=spt[:, d, :], in0=spw[:, d, :], scalar=-1.0,
                                            in1=spe[:, d, :], op0=ALU.add, op1=ALU.subtract).then_inc(s_spt, 1)
                dv.wait_ge(s_spz, (c + 1) * ND)
                for d in range(2, ND):
                    dv.wait_ge(s_spt, c * ND + d + 1)
                    fr.done(dv.tensor_tensor(spt[:, d, :], delta[:, d, :], spt[:, d, :], ALU.subtract))
                for d in range(ND):
                    if d < 2:
                        dv.wait_ge(s_spr, c * 2 + d + 1)
                    else:
                        dv.wait_ge(s_v, fr.before + fr.steps - (ND - 1) + d)
                    dv.wait_ge(s_spl, c * ND + d + 1)
                    dv.tensor_tensor(delta[:, d, :], spt[:, d, :], spl[:, d, :], ALU.add).then_inc(s_dl, 1)
                for d in range(2, ND):
                    dv.wait_ge(s_dl, c * ND + d + 1)
                    dv.tensor_tensor(du[:, d, :], delta[:, d, :], u[:, d, :], ALU.mult).then_inc(s_du, 1)
                dv.wait_ge(s_xst, NC * 16)
                for k in range(2, 4):
                    add_out(1 - cc % 2, k, c * 4 + k)
                assert fr.steps == VFRONT + VCONV, fr.steps
                dv.wait_ge(s_du, (c + 1) * 2)
                dv.wait_ge(s_dup, (c + 1) * 2)
                dv.wait_ge(s_st, c * NG * ND + H2)
                for n, g, q, pair in groups(dv, c):
                    dv.wait_ge(s_bcl[q], (pair + 1) * 32)
                    drive(0, g, q)
                    drive(1, g, q)
                    output_rows(1 - q, g)
                    take_rows(q, pair)
                    scan(0, g, n)
                    scan(1, g, n)
                    dv.wait_ge(s_h, g * ND + 1 + CR)
                    drive(2, g, q)
                    keep(0, g, n)
                    dv.wait_ge(s_h, g * ND + 2 + CR)
                    drive(3, g, q)
                    keep(1, g, n)
                    scan(2, g, n)
                    scan(3, g, n)
                    keep(2, g, n)
                    dv.wait_ge(s_mf, (g + 1) * 2)
                    dv.wait_ge(s_mg, g + 1)
                    for f in range(NF):
                        a = act[q][:, f, 0:ST]
                        m = dv.scalar_tensor_tensor(out=a, in0=fh[2][:, f * ST:(f + 1) * ST],
                                                    scalar=wp[q][:, B1 + f:B1 + f + 1], in1=a, op0=ALU.add,
                                                    op1=ALU.mult)
                    m.then_inc(s_ma, 1)
                    dv.wait_ge(s_h, (g + 1) * ND + CR)
                    dv.wait_ge(s_ns, g * ND + CR)
                    dv.tensor_tensor(hC[2], h[1], Cb[q], ALU.mult).then_inc(s_hCv, 1)
                    keep(3, g, n)
                for d in range(ND):
                    dv.wait_ge(s_ns, (c + 1) * NG * ND - (ND - 1) + d + CR)
                    dv.tensor_tensor(gated[:, d, :], sres[:, d, :], y[d][:, :], ALU.mult).then_inc(s_yg, 1)
            dv.wait_ge(s_col, SLOT_TILES + HS)
            output_rows(1, SLOT_TILES)
            for k in range(2, 4):
                add_out(1, k, NC * 4 + k - 2)
            for c, q, turn in pairs(dv):
                dv.wait_ge(s_xa[q], (turn + (1 + NC)) * 16)
                dv.wait_ge(s_gy[q], (turn + 1) * (TOPK * 16))
                for k in range(TOPK):
                    if k:
                        dv.wait_ge(s_gv, c * ((TOPK - 1) * NT) + k * NT)
                    for t in range(NT):
                        row = xa[:, q, t, :]
                        m = dv.scalar_tensor_tensor(out=row, in0=gy[q][:, k * NT + t, :],
                                                    scalar=wk[:, bass.ds(c * (TOPK * NT) + k * NT + t, 1)], in1=row,
                                                    op0=ALU.mult, op1=ALU.add)
                        if k < TOPK - 1:
                            m.then_inc(s_gv, 1)
                        elif t == NT - 1:
                            m.then_inc(s_ga, 1)


def kernel(**inputs):
    import numpy as _np
    import concourse.bacc as _bacc
    from concourse import mybir as _mybir
    from concourse.bass_utils import run_bass_kernel_spmd as _run

    a = {k[3:]: _np.asarray(v) for k, v in inputs.items()}
    P = 128
    E = a["ffn_gate_w"].shape[0]
    DM = a["attn_x"].shape[2]
    F = a["ffn_fc2_w"].shape[2]
    FS = a["ffn_s_fc2_w"].shape[1]

    def parts(m):
        return _np.ascontiguousarray(_np.swapaxes(m.reshape(m.shape[0] // P, P, *m.shape[1:]), 0, 1))

    def half(m, lo, axis=0):
        return _np.take(m, range(lo, lo + F), axis=axis)

    s1, s1b = a["ffn_s_fc1_w"], a["ffn_s_fc1_b"]
    fc1 = [m for m in a["ffn_fc1_w"]]
    fc1_b = [m for m in a["ffn_fc1_b"]]
    mult = [m for m in a["ffn_geglu_mult"]]
    fc2 = [m for m in a["ffn_fc2_w"]]
    for lo in range(0, FS, F):
        fc1.append(_np.concatenate([half(s1, lo), half(s1, FS + lo)]))
        fc1_b.append(_np.concatenate([half(s1b, lo), half(s1b, FS + lo)]))
        mult.append(half(a["ffn_s_geglu_mult"], lo))
        fc2.append(half(a["ffn_s_fc2_w"], lo, 1))

    def columns(vectors):
        v = _np.stack(vectors)
        return _np.ascontiguousarray(v.reshape(-1, P).T)

    def pack(w1, w2, b, m):
        return _np.concatenate([parts(_np.ascontiguousarray(w1.T)).reshape(P, -1),
                                columns([b]), parts(_np.ascontiguousarray(w2.T)).reshape(P, -1), columns([m])], 1)

    T = a["attn_x"].shape[0] * a["attn_x"].shape[1] // P
    restart = _np.ones((P, E, T), _np.float32)
    restart[:, :, 0] = 0
    TOPK, NT, TRASH = 3, 4, 512
    p, c, k, t = _np.ogrid[:P, :T // NT, :TOPK, :NT]
    rows = _np.concatenate([(TRASH + k * T * P + (c * NT + t) * P + p).reshape(P, -1),
                            _np.arange(P)[:, None] + P * _np.arange(TRASH // P)], 1).astype(_np.float32)
    data = {
        "x": a["attn_x"], "w_in": parts(a["attn_W_in"]),
        "conv_w": parts(_np.ascontiguousarray(a["attn_conv_w"][:, 0, :].T)), "conv_b": columns([a["attn_conv_b"]]),
        "w_x": parts(a["attn_W_x"]), "w_dt": a["attn_W_dt"], "b_dt": columns([a["attn_b_dt"]]),
        "a_log": parts(a["attn_A_log"]).reshape(P, -1), "d_skip": columns([a["attn_D"]]), "w_out": parts(a["attn_W_out"]),
        "gate_w": parts(_np.ascontiguousarray(a["ffn_gate_w"].T)),
        "packs": _np.stack([pack(*unit) for unit in zip(fc1, fc2, fc1_b, mult)]),
        "fc2_b": _np.concatenate([a["ffn_fc2_b"], a["ffn_s_fc2_b"][None]]),
        "ident": _np.eye(P, dtype=_np.float32),
        "tri": _np.triu(_np.ones((P, P), _np.float32), 1),
        "prio": _np.tile(_np.arange(E, 0, -1, dtype=_np.float32), (P, T)),
        "restart": restart.reshape(P, -1), "tiles": _np.tile(_np.arange(64, dtype=_np.float32), (P, 1)),
        "rows": rows,
    }
    nc = _bacc.Bacc("TRN2", target_bir_lowering=False, num_devices=1)
    arrays, args = {}, []
    for name, v in data.items():
        v = _np.ascontiguousarray(v)
        arrays[f"in_{name}"] = v
        args.append(nc.dram_tensor(f"in_{name}", v.shape, _mybir.dt.from_np(v.dtype), kind="ExternalInput").ap())
    args.append(nc.dram_tensor("out", a["attn_x"].shape, _mybir.dt.float32, kind="ExternalOutput").ap())
    mamba_moe_block(nc, *args)
    r = _run(nc, [arrays], core_ids=[0])
    return r.results[0]["out"]
```
